# Optimizing a Trainium2 kernel written in Bass

```python
import numpy as np
import jax
import jax.numpy as jnp

def _softmax(x, axis=-1):
    return jax.nn.softmax(x, axis=axis)

def _gelu(x):
    return jax.nn.gelu(x, approximate=True)

def _silu(x):
    return jax.nn.silu(x)

def _sigmoid(x):
    return jax.nn.sigmoid(x)

def _layernorm(x, axis=-1, eps=1e-05):
    m = jnp.mean(x, axis=axis, keepdims=True)
    v = jnp.var(x, axis=axis, keepdims=True)
    return (x - m) / jnp.sqrt(v + eps)

def _scatter_add(tgt, idx, src, axis=0):
    return tgt.at[idx].add(src)

def _segment_sum(src, seg, n):
    return jax.ops.segment_sum(src, seg, n)
kernel_name = 'mk_conv_seq_d2_conv_nchw256_r4_0afe26'

def setup_inputs(seed: int=0):
    np.random.seed(seed)
    _w = jnp.asarray

    def _rec_inputs():
        import jax
        import jax.numpy as jnp
        _gk = jax.random.key(seed)
        x = -0.0003957 + 1 * jax.random.normal(jax.random.fold_in(_gk, 1), (16, 64, 56, 56), jnp.float32)
        return x
    x = _rec_inputs()

    def _L0_conv_setup():
        import jax, jax.numpy as jnp
        import numpy as np
        B, C, RES, WS, HEADS, GROUPS, MLP_DIM = (16, 64, 56, 7, 8, 16, 256)
        HEAD_DIM = C // HEADS
        N = WS * WS

        def _rel_index(ws):
            coords = np.stack(np.meshgrid(np.arange(ws), np.arange(ws), indexing='ij'), 0).reshape(2, -1)
            rel = (coords[:, :, None] - coords[:, None, :]).transpose(1, 2, 0) + ws - 1
            return jnp.asarray(rel[..., 0] * (2 * ws - 1) + rel[..., 1], jnp.int32)

        def _group_norm(x, w, b, groups, eps=1e-05):
            bn, c, h, ww = x.shape
            xg = x.reshape(bn, groups, c // groups, h, ww)
            m = xg.mean((2, 3, 4), keepdims=True)
            v = xg.var((2, 3, 4), keepdims=True)
            xg = (xg - m) * jax.lax.rsqrt(v + eps)
            return xg.reshape(bn, c, h, ww) * w[None, :, None, None] + b[None, :, None, None]

        def _window_cosine_attn(x, qkv_w, qkv_b, logit_scale, bias_table, rel_index, proj_w, proj_b):
            bn, c, hh, ww = x.shape
            nh, nw = (hh // WS, ww // WS)
            xw = x.reshape(bn, c, nh, WS, nw, WS).transpose(0, 2, 4, 3, 5, 1).reshape(bn * nh * nw, N, c)
            qkv = xw @ qkv_w.T + qkv_b
            qkv = qkv.reshape(-1, N, 3, HEADS, HEAD_DIM).transpose(2, 0, 3, 1, 4)
            q, k, v = (qkv[0], qkv[1], qkv[2])
            qn = q / jnp.clip(jnp.linalg.norm(q, axis=-1, keepdims=True), 1e-12)
            kn = k / jnp.clip(jnp.linalg.norm(k, axis=-1, keepdims=True), 1e-12)
            scale = jnp.exp(jnp.minimum(logit_scale, jnp.log(100.0)))[None, :, None, None]
            attn = jnp.einsum('bhnd,bhmd->bhnm', qn, kn) * scale
            bias = bias_table[rel_index].transpose(2, 0, 1)
            attn = jax.nn.softmax(attn + bias[None], axis=-1)
            out = jnp.einsum('bhnm,bhmd->bhnd', attn, v)
            out = out.transpose(0, 2, 1, 3).reshape(-1, N, c) @ proj_w.T + proj_b
            out = out.reshape(bn, nh, nw, WS, WS, c).transpose(0, 5, 1, 3, 2, 4).reshape(bn, c, hh, ww)
            return out
        key = jax.random.key(seed)
        ks = jax.random.split(key, 8)
        s = 0.02
        return {'x': jax.random.normal(ks[0], (B, C, RES, RES), jnp.float32), 'qkv_w': jax.random.normal(ks[1], (3 * C, C), jnp.float32) * s, 'qkv_b': jnp.zeros((3 * C,), jnp.float32), 'logit_scale': jnp.full((HEADS,), np.log(10.0), jnp.float32), 'bias_table': jax.random.normal(ks[2], ((2 * WS - 1) ** 2, HEADS), jnp.float32) * s, 'rel_index': _rel_index(WS), 'proj_w': jax.random.normal(ks[3], (C, C), jnp.float32) * s, 'proj_b': jnp.zeros((C,), jnp.float32), 'gn1_w': jnp.ones((C,), jnp.float32), 'gn1_b': jnp.zeros((C,), jnp.float32), 'gn2_w': jnp.ones((C,), jnp.float32), 'gn2_b': jnp.zeros((C,), jnp.float32), 'mlp_gn_w': jnp.ones((C,), jnp.float32), 'mlp_gn_b': jnp.zeros((C,), jnp.float32), 'mlp_w1': jax.random.normal(ks[4], (MLP_DIM, C), jnp.float32) * s, 'mlp_b1': jnp.zeros((MLP_DIM,), jnp.float32), 'mlp_w2': jax.random.normal(ks[5], (C, MLP_DIM), jnp.float32) * s, 'mlp_b2': jnp.zeros((C,), jnp.float32)}
    _L0_conv_all = _L0_conv_setup()
    _L0_conv_in = {k: v for k, v in _L0_conv_all.items() if k in ('qkv_w', 'qkv_b', 'logit_scale', 'bias_table', 'rel_index', 'proj_w', 'proj_b', 'gn1_w', 'gn1_b', 'gn2_w', 'gn2_b', 'mlp_gn_w', 'mlp_gn_b', 'mlp_w1', 'mlp_b1', 'mlp_w2', 'mlp_b2')}
    del _L0_conv_all

    def _L1_conv_setup():
        import jax, jax.numpy as jnp
        import numpy as np
        HEADS = 4
        key = jax.random.key(seed)
        k1, k2, k3 = jax.random.split(key, 3)
        b, c, h, w = (4, 64, 16, 16)
        x = jax.random.normal(k1, (b, c, h, w), dtype=jnp.float32)
        w_qkv = jax.random.normal(k2, (3 * c, c), dtype=jnp.float32) * c ** (-0.5)
        w_proj = jax.random.normal(k3, (c, c), dtype=jnp.float32) * c ** (-0.5)
        return {'x': x, 'w_qkv': w_qkv, 'w_proj': w_proj}
    _L1_conv_all = _L1_conv_setup()
    _L1_conv_in = {k: v for k, v in _L1_conv_all.items() if k in ('w_qkv', 'w_proj')}
    del _L1_conv_all
    return {'x': x, 'L0_conv_qkv_w': _L0_conv_in['qkv_w'], 'L0_conv_qkv_b': _L0_conv_in['qkv_b'], 'L0_conv_logit_scale': _L0_conv_in['logit_scale'], 'L0_conv_bias_table': _L0_conv_in['bias_table'], 'L0_conv_rel_index': _L0_conv_in['rel_index'], 'L0_conv_proj_w': _L0_conv_in['proj_w'], 'L0_conv_proj_b': _L0_conv_in['proj_b'], 'L0_conv_gn1_w': _L0_conv_in['gn1_w'], 'L0_conv_gn1_b': _L0_conv_in['gn1_b'], 'L0_conv_gn2_w': _L0_conv_in['gn2_w'], 'L0_conv_gn2_b': _L0_conv_in['gn2_b'], 'L0_conv_mlp_gn_w': _L0_conv_in['mlp_gn_w'], 'L0_conv_mlp_gn_b': _L0_conv_in['mlp_gn_b'], 'L0_conv_mlp_w1': _L0_conv_in['mlp_w1'], 'L0_conv_mlp_b1': _L0_conv_in['mlp_b1'], 'L0_conv_mlp_w2': _L0_conv_in['mlp_w2'], 'L0_conv_mlp_b2': _L0_conv_in['mlp_b2'], 'L1_conv_w_qkv': _L1_conv_in['w_qkv'], 'L1_conv_w_proj': _L1_conv_in['w_proj']}

def reference(x, L0_conv_qkv_w, L0_conv_qkv_b, L0_conv_logit_scale, L0_conv_bias_table, L0_conv_rel_index, L0_conv_proj_w, L0_conv_proj_b, L0_conv_gn1_w, L0_conv_gn1_b, L0_conv_gn2_w, L0_conv_gn2_b, L0_conv_mlp_gn_w, L0_conv_mlp_gn_b, L0_conv_mlp_w1, L0_conv_mlp_b1, L0_conv_mlp_w2, L0_conv_mlp_b2, L1_conv_w_qkv, L1_conv_w_proj):
    import jax
    import jax.numpy as jnp

    def _L0_conv_ref(x, qkv_w, qkv_b, logit_scale, bias_table, rel_index, proj_w, proj_b, gn1_w, gn1_b, gn2_w, gn2_b, mlp_gn_w, mlp_gn_b, mlp_w1, mlp_b1, mlp_w2, mlp_b2):
        import jax, jax.numpy as jnp
        import numpy as np
        B, C, RES, WS, HEADS, GROUPS, MLP_DIM = (16, 64, 56, 7, 8, 16, 256)
        HEAD_DIM = C // HEADS
        N = WS * WS

        def _rel_index(ws):
            coords = np.stack(np.meshgrid(np.arange(ws), np.arange(ws), indexing='ij'), 0).reshape(2, -1)
            rel = (coords[:, :, None] - coords[:, None, :]).transpose(1, 2, 0) + ws - 1
            return jnp.asarray(rel[..., 0] * (2 * ws - 1) + rel[..., 1], jnp.int32)

        def _group_norm(x, w, b, groups, eps=1e-05):
            bn, c, h, ww = x.shape
            xg = x.reshape(bn, groups, c // groups, h, ww)
            m = xg.mean((2, 3, 4), keepdims=True)
            v = xg.var((2, 3, 4), keepdims=True)
            xg = (xg - m) * jax.lax.rsqrt(v + eps)
            return xg.reshape(bn, c, h, ww) * w[None, :, None, None] + b[None, :, None, None]

        def _window_cosine_attn(x, qkv_w, qkv_b, logit_scale, bias_table, rel_index, proj_w, proj_b):
            bn, c, hh, ww = x.shape
            nh, nw = (hh // WS, ww // WS)
            xw = x.reshape(bn, c, nh, WS, nw, WS).transpose(0, 2, 4, 3, 5, 1).reshape(bn * nh * nw, N, c)
            qkv = xw @ qkv_w.T + qkv_b
            qkv = qkv.reshape(-1, N, 3, HEADS, HEAD_DIM).transpose(2, 0, 3, 1, 4)
            q, k, v = (qkv[0], qkv[1], qkv[2])
            qn = q / jnp.clip(jnp.linalg.norm(q, axis=-1, keepdims=True), 1e-12)
            kn = k / jnp.clip(jnp.linalg.norm(k, axis=-1, keepdims=True), 1e-12)
            scale = jnp.exp(jnp.minimum(logit_scale, jnp.log(100.0)))[None, :, None, None]
            attn = jnp.einsum('bhnd,bhmd->bhnm', qn, kn) * scale
            bias = bias_table[rel_index].transpose(2, 0, 1)
            attn = jax.nn.softmax(attn + bias[None], axis=-1)
            out = jnp.einsum('bhnm,bhmd->bhnd', attn, v)
            out = out.transpose(0, 2, 1, 3).reshape(-1, N, c) @ proj_w.T + proj_b
            out = out.reshape(bn, nh, nw, WS, WS, c).transpose(0, 5, 1, 3, 2, 4).reshape(bn, c, hh, ww)
            return out
        h = _window_cosine_attn(x, qkv_w, qkv_b, logit_scale, bias_table, rel_index, proj_w, proj_b)
        h = jax.nn.relu(_group_norm(x + h, gn1_w, gn1_b, GROUPS))
        m = _group_norm(h, mlp_gn_w, mlp_gn_b, GROUPS)
        m = jax.nn.relu(jnp.einsum('bchw,ec->behw', m, mlp_w1) + mlp_b1[None, :, None, None])
        m = jnp.einsum('behw,ce->bchw', m, mlp_w2) + mlp_b2[None, :, None, None]
        z = jax.nn.relu(_group_norm(h + m, gn2_w, gn2_b, GROUPS))
        return z

    def _L1_conv_ref(x, w_qkv, w_proj):
        import jax, jax.numpy as jnp
        import numpy as np
        HEADS = 4
        b, c, h, w = x.shape
        heads = HEADS
        d = c // heads
        scale = d ** (-0.5)
        n = h * w
        qkv = jnp.einsum('oc,bchw->bohw', w_qkv, x)
        q, k, v = jnp.split(qkv.reshape(b, 3 * c, n), 3, axis=1)
        q = q.reshape(b, heads, d, n)
        k = k.reshape(b, heads, d, n)
        v = v.reshape(b, heads, d, n)
        attn = jax.nn.softmax(jnp.einsum('bhdn,bhdm->bhnm', q, k) * scale, axis=-1)
        out = jnp.einsum('bhnm,bhdm->bhdn', attn, v).reshape(b, c, h, w)
        return jnp.einsum('oc,bchw->bohw', w_proj, out) + x

    def _gn(v, G=32, eps=1e-05):
        B_, C_, H_, W_ = v.shape
        g = v.reshape(B_, G, C_ // G, H_, W_)
        m = jnp.mean(g, axis=(2, 3, 4), keepdims=True)
        s = jnp.var(g, axis=(2, 3, 4), keepdims=True)
        return ((g - m) / jnp.sqrt(s + eps)).reshape(v.shape)

    def _ln_c(v, eps=1e-06):
        m = jnp.mean(v, axis=1, keepdims=True)
        s = jnp.var(v, axis=1, keepdims=True)
        return (v - m) / jnp.sqrt(s + eps)

    def _ln_t(v, eps=1e-05):
        m = jnp.mean(v, axis=-1, keepdims=True)
        s = jnp.var(v, axis=-1, keepdims=True)
        return (v - m) / jnp.sqrt(s + eps)

    def _to_tokens(v):
        B_, C_, H_, W_ = v.shape
        return v.reshape(B_, C_, H_ * W_).transpose(0, 2, 1)

    def _from_tokens(t, like):
        B_, C_, H_, W_ = like.shape
        return t.transpose(0, 2, 1).reshape(B_, C_, H_, W_)
    x = _L0_conv_ref(x, L0_conv_qkv_w, L0_conv_qkv_b, L0_conv_logit_scale, L0_conv_bias_table, L0_conv_rel_index, L0_conv_proj_w, L0_conv_proj_b, L0_conv_gn1_w, L0_conv_gn1_b, L0_conv_gn2_w, L0_conv_gn2_b, L0_conv_mlp_gn_w, L0_conv_mlp_gn_b, L0_conv_mlp_w1, L0_conv_mlp_b1, L0_conv_mlp_w2, L0_conv_mlp_b2)
    x = _L1_conv_ref(x, L1_conv_w_qkv, L1_conv_w_proj)
    return x

_drawn_inputs = setup_inputs


def setup_inputs(seed=0):
    import zlib

    import numpy as np

    out = dict(_drawn_inputs(seed))
    spreads = {'L0_conv_qkv_b': (0.0, 0.363),
     'L0_conv_logit_scale': (2.3025851249694824, 0.6),
     'L0_conv_proj_b': (0.0, 0.1),
     'L0_conv_gn1_w': (1.0, 0.2),
     'L0_conv_gn1_b': (0.0, 0.1),
     'L0_conv_gn2_w': (1.0, 0.2),
     'L0_conv_gn2_b': (0.0, 0.1),
     'L0_conv_mlp_gn_w': (1.0, 0.6),
     'L0_conv_mlp_gn_b': (0.0, 2.0),
     'L0_conv_mlp_b1': (0.0, 0.38),
     'L0_conv_mlp_b2': (0.0, 0.1)}
    factors = {'L0_conv_qkv_w': 3.373, 'L0_conv_bias_table': 64.0}
    for name, (base, spread) in spreads.items():
        noise = np.random.default_rng([zlib.crc32(name.encode()), seed]).standard_normal(out[name].shape)
        drawn = base * np.exp(spread * noise) if base else spread * noise
        out[name] = jnp.asarray(drawn.astype(out[name].dtype))
    for name, factor in factors.items():
        out[name] = (out[name] * factor).astype(out[name].dtype)
    return out
```

```python
import concourse.bass as bass
from concourse import mybir
from contextlib import ExitStack

IMAGES, CH, RES, WIN = 16, 64, 56, 7
TOKENS = RES * RES
NWIN = (RES // WIN) ** 2
WTOK = WIN * WIN
GROUPS = RES // WIN
GTOK = TOKENS // GROUPS
H0, D0 = 8, 8
H1, D1 = 4, 16
HID = 256
TABLE = (2 * WIN - 1) ** 2
TILES = -(-TOKENS // 128)
PADTOK = TILES * 128
PAIR = 2 * GTOK
PIECES = 6
STACK = PIECES * D1
SHIFT = 3
EXP_UNITS = 2 * TILES * 2
MAX_UNITS = TILES * 4
LN100 = 4.605170185988092


def attention_mlp_kernel(nc, x, qkv0, qkv0_b, logit_scale, table, rel_index, proj0, proj0_b, gn1_w, gn1_b,
                         gn2_w, gn2_b, gnm_w, gnm_b, w1, b1, w2, b2, qkv1, proj1,
                         ident, head_sum, group_mean, head_mask, rows, out, scratch_bias, scratch_att, scratch_den,
                         scratch_rden):
    f32, bf16, i32 = mybir.dt.float32, mybir.dt.bfloat16, mybir.dt.int32
    ALU, ACT, AX = mybir.AluOpType, mybir.ActivationFunctionType, mybir.AxisListType

    ctx = ExitStack()
    with ctx:
        def sb(name, shape, dt=f32):
            return ctx.enter_context(nc.sbuf_tensor(name, shape, dt))

        def sem(name):
            return ctx.enter_context(nc.semaphore(name))

        w_qk0 = sb("w_qk0", [CH, 128])
        w_v0 = sb("w_v0", [CH, CH])
        w_p0 = sb("w_p0", [128, CH])
        w_p0c = sb("w_p0c", [CH, CH])
        w_1 = sb("w_1", [CH, HID])
        w_2 = sb("w_2", [128, 2, CH])
        w_qk1 = sb("w_qk1", [CH, 128])
        w_v1 = sb("w_v1", [CH, CH])
        w_p1 = sb("w_p1", [CH, CH])
        vec = sb("vec", [128, 24])
        bqk0, pb0, bv0, b2c = vec[:, 0:1], vec[0:CH, 1:2], vec[0:CH, 2:3], vec[0:CH, 3:4]
        b1c = [vec[:, 4:5], vec[:, 5:6]]
        gn_w = [vec[0:CH, 6 + 2 * i:7 + 2 * i] for i in range(3)]
        gn_b = [vec[0:CH, 7 + 2 * i:8 + 2 * i] for i in range(3)]
        qkscale, rows_c = vec[:, 12:13], vec[:, 13:15]
        scale_raw, minus_half = vec[:, 15:16], vec[:, 16:17]
        pbias = vec[0:CH, 17:18]
        idf = sb("idf", [128, 128])
        idb = sb("idb", [128, 128], bf16)
        hsum = sb("hsum", [128, 128])
        gmean = sb("gmean", [CH, CH])
        vmask = sb("vmask", [2 * WTOK, 2 * D0])
        tab = sb("tab", [128, 2, H0])
        bias = sb("bias", [128, H0 * WTOK])

        x_in = sb("x_in", [CH, TOKENS])
        x_w = sb("x_w", [CH, PADTOK])
        T2 = sb("T2", [128, TOKENS])
        T3 = sb("T3", [128, TOKENS])
        T4 = sb("T4", [128, PADTOK])
        z_w = sb("z_w", [CH, PADTOK])
        kmask = sb("kmask", [CH, 2, H0, GTOK])
        SP_ = sb("SPx", [128, 4, PAIR])
        PV_ = sb("PVx", [128, 2, 4, 512])
        VB = sb("VB", [2 * WTOK, 2, 8, 4, 32])
        piece_l = sb("piece_l", [128, TOKENS], bf16)
        pieces = [T2[:, :].bitcast(bf16)[:, 0:TOKENS], T2[:, :].bitcast(bf16)[:, TOKENS:2 * TOKENS], piece_l[:, :]]
        QS = sb("QS", [128, H1, PADTOK], bf16)
        KS = sb("KS", [128, H1, PADTOK], bf16)
        small = sb("small", [128, 256])
        nmt = sb("nmt", [3 * TILES, 128], bf16)
        nmp = sb("nmp", [128, 3, TILES], bf16)
        o_st = T2[:, 0:2 * GTOK].rearrange("p (a n) -> p a n", a=2)

        Sb = SP_[:, :, :].rearrange("p a n -> p (a n)").rearrange("p (b c n) -> p b c n", b=2, c=4)
        Sb = SP_[:, :, :].rearrange("p (b c) n -> p b (c n)", b=2)
        hid = SP_[:, :, :]
        E = SP_[:, :, :]
        PT = PV_
        v_all = PV_[:, :, :, :].rearrange("p a b n -> p (a b n)")[:, 0:H1 * TILES * 32]
        v_all = v_all.rearrange("p (h t c) -> p h t c", h=H1, t=TILES)
        v_all_flat = PV_[:, :, :, :].rearrange("p a b n -> p (a b n)")
        QF = QS[:, :, :].rearrange("p h n -> p (h n)")
        KF = KS[:, :, :].rearrange("p h n -> p (h n)")
        x_tw = sb("x_tw", [CH, 2, 8, 2, WTOK])
        v_h = v_all_flat[:, H1 * TILES * 32:(H1 + 1) * TILES * 32].rearrange("p (t c) -> p t c", c=32)
        nmx, den, rden = small[:, 0:32], small[:, 32:64], small[:, 64:96]
        stats = small[0:CH, 96:144].rearrange("p (c s) -> p c s", c=8)
        mv, gd, ge, gt, gp, gA, gB = (small[0:CH, 144 + 4 * i:146 + 4 * i] for i in range(7))
        mxp = small[:, 0:100]
        nm = small[:, 100:125]
        nr = small[:, 125:150]
        dcomp = small[:, 0:98]
        rdcomp = small[:, 98:196]

        PS = ctx.enter_context(nc.psum_tensor("PS", [128, 8, 512], f32))

        s_w, s_k = sem("weights_loaded"), sem("scale_loaded")
        s_i0, s_i1, s_i2, s_i3, s_i4, s_i5, s_i6 = (sem(f"setup{i}") for i in range(7))
        s_bd, s_bl = sem("bias_stored"), sem("bias_loaded")
        s_setup = sem("setup_chain")
        s_xin, s_xw, s_x2 = sem("x_loaded"), sem("x_by_windows"), sem("x_twice")
        s_qk, s_sq, s_ssq, s_max, s_root, s_qn = (sem(n) for n in (
            "qk_product", "qk_squares", "head_sums", "sums_bounded", "roots", "qk_normalised"))
        s_km = [sem("kmask_even"), sem("kmask_odd")]
        s_S, s_add, s_sub, s_exp0, s_P, s_V, s_vb = (sem(n) for n in (
            "win_scores", "win_biased", "win_shifted", "win_exps", "win_probs", "win_v", "win_v_blocks"))
        s_T, s_PT, s_PV, s_at, s_pr, s_h1 = (sem(n) for n in (
            "win_transposed", "win_transposed_copied", "win_pv", "win_att", "win_proj", "residual1"))
        s_gq, s_gr, s_pq, s_pw, s_af = (sem(n) for n in (
            "gn_request", "gn_mean", "pow_request", "pow_done", "gn_affine"))
        s_h, s_mi, s_m1, s_hid, s_m2, s_h2, s_z = (sem(n) for n in (
            "h_ready", "mlp_in", "mlp1", "hidden", "mlp2", "residual2", "z_ready"))
        s_gqk, s_ph, s_r, s_pm, s_pl, s_gv, s_va, s_ones = (sem(n) for n in (
            "gqk", "piece_h", "rest", "piece_m", "piece_l", "gv", "v_all_ready", "ones_set"))
        s_st = sem("stacks_loaded")
        s_mx, s_mu, s_nm, s_nt, s_nc, s_sh = (sem(n) for n in (
            "max_scores", "max_taken", "max_pieces", "max_transposed", "max_copied", "shift_loaded"))
        s_vh, s_gs, s_ex, s_gpv, s_o, s_od = (sem(n) for n in (
            "v_head", "scores", "exps", "pv_done", "out_copied", "out_stored"))
        s_al, s_dl, s_dr, s_ds, s_rl, s_ao, s_fp, s_fin, s_out = (sem(n) for n in (
            "att_loaded", "den_loaded", "den_inverted", "rden_stored", "rden_loaded", "att_scaled",
            "final_proj", "final", "out_written"))
        s_cd, s_ch, s_cf = sem("dve_chain"), sem("dve_head_chain"), sem("dve_final_chain")
        CD = 64

        def wait_apart(eng, semaphore, value):
            value = eng.to_reg(value)
            eng.wait_ge(s_i1, 9)
            eng.wait_ge(semaphore, value)

        block = ctx.enter_context(nc.Block())
        NLOAD = 32

        @block.sync
        def _(sp):
            def load(dst, src, s=s_w):
                sp.dma_start(dst, src).then_inc(s, 16)

            col = lambda v: v.rearrange("(n o) -> n o", o=1)
            load(T3[:, 0:WTOK * WTOK].bitcast(i32), rel_index.rearrange("n m -> (n m)").partition_broadcast(128))
            load(tab[:, 0, :], table[0:128, :])
            load(tab[0:TABLE - 128, 1, :], table[128:TABLE, :])
            load(rows_c, rows)
            load(w_qk0[:], qkv0[:, 0:128])
            load(w_v0[:], qkv0[:, 128:192])
            sp.wait_ge(s_i0, 2)
            for p in range(4):
                load(w_p0[32 * p:32 * p + 16, :], proj0[16 * p:16 * p + 16, :])
            load(w_p0c[:], proj0)
            load(w_1[:], w1)
            load(w_2[:], w2.rearrange("(a p) c -> p a c", a=2))
            load(w_qk1[:], qkv1[:, 0:128])
            load(w_v1[:], qkv1[:, 128:192])
            load(w_p1[:], proj1)
            load(bqk0, col(qkv0_b[0:128]))
            load(bv0, col(qkv0_b[128:192]))
            load(pb0, col(proj0_b))
            load(b2c, col(b2))
            load(b1c[0], col(b1[0:128]))
            load(b1c[1], col(b1[128:256]))
            for i, (w_, b_) in enumerate(((gn1_w, gn1_b), (gnm_w, gnm_b), (gn2_w, gn2_b))):
                load(gn_w[i], col(w_))
                load(gn_b[i], col(b_))
            load(idf[:], ident)
            load(hsum[:], head_sum)
            load(gmean[:], group_mean)
            load(vmask[:], head_mask)
            for h in range(H0):
                load(scale_raw[CH + D0 * h:CH + D0 * h + D0, :],
                     logit_scale[h:h + 1].partition_broadcast(D0), s_k)
            sp.wait_ge(s_i4, 7)
            sp.dma_start(scratch_bias, T4[0:H0, 0:WTOK * WTOK]).then_inc(s_bd, 16)
            sp.wait_ge(s_bd, 16)
            sp.wait_ge(s_i0, 2)
            for q in range(2):
                sp.dma_start(bias[64 * q:64 * q + WTOK, :].rearrange("n (h m) -> n h m", h=H0),
                             scratch_bias.rearrange("h (n m) -> n h m", n=WTOK)).then_inc((s_bl, s_out)[q], 16)
            sp.dma_start(x_in[:], x[0, :, :]).then_inc(s_xin, 16)

            with sp.Fori(0, IMAGES) as b:
                sp.wait_ge(s_xw, b * 8 + 8)
                sp.dma_start(x_in[:], x[bass.ds((b + 1) % IMAGES, 1), :, :].rearrange("o c n -> (o c) n"))\
                  .then_inc(s_xin, 16)
                for g in range(GROUPS):
                    sp.wait_ge(s_qn, b * 4 + g // 2 + 1)
                    if g >= 2:
                        sp.wait_ge(s_S, b * 8 + g - 1)
                    for h in range(H0):
                        sp.dma_start(kmask[D0 * h:D0 * h + D0, g % 2, h, :],
                                     T4[CH + D0 * h:CH + D0 * h + D0, g * GTOK:(g + 1) * GTOK])\
                          .then_inc(s_km[g % 2], 16)
                sp.wait_ge(s_pl, b * 4 + 4)
                sp.wait_ge(s_pm, b * 4 + 4)
                for h in range(H1):
                    for dst, base, order in ((QS, 0, (0, 0, 1, 1, 0, 2)), (KS, CH, (0, 1, 0, 1, 2, 0))):
                        for j, pc in enumerate(order):
                            sp.dma_start(dst[D1 * j:D1 * j + D1, h, 0:TOKENS],
                                         pieces[pc][base + D1 * h:base + D1 * h + D1, :]).then_inc(s_st, 16)
                with sp.Fori(0, H1) as h:
                    hd = b * H1 + h
                    sp.wait_ge(s_nc, hd + 1)
                    for pc in range(3):
                        sp.dma_start(QF[STACK + pc:STACK + pc + 1, bass.ds(h * PADTOK, PADTOK)]
                                     .rearrange("p (t n) -> p t n", n=128),
                                     nmt[TILES * pc:TILES * pc + TILES, :]).then_inc(s_sh, 16)
                    for half in range(2):
                        sp.wait_ge(s_o, hd * 2 + half + 1)
                        for j in range(4):
                            c0 = (4 * half + j) * GTOK
                            sp.dma_start(scratch_att[bass.ds(h * D1, D1), c0:c0 + GTOK],
                                         o_st[32 * j:32 * j + D1, half, :]).then_inc(s_od, 16)
                            sp.dma_start(scratch_den[bass.ds(h, 1), c0:c0 + GTOK],
                                         o_st[32 * j + D1:32 * j + D1 + 1, half, :]).then_inc(s_od, 16)
                    wait_apart(sp, s_od, hd * 256 + 256)
                sp.dma_start(dcomp, scratch_den.rearrange("h (a n) -> (h a) n", a=32)).then_inc(s_dl, 16)
                sp.dma_start(T4[0:CH, 0:TOKENS], scratch_att).then_inc(s_al, 16)
                sp.wait_ge(s_dr, b + 1)
                sp.dma_start(scratch_rden.rearrange("h (a n) -> (h a) n", a=32), rdcomp).then_inc(s_ds, 16)
                sp.wait_ge(s_ds, b * 16 + 16)
                for h in range(H1):
                    sp.dma_start(T3[D1 * h:D1 * h + D1, 0:TOKENS], scratch_rden[h, :].partition_broadcast(D1))\
                      .then_inc(s_rl, 16)
                sp.wait_ge(s_fin, b * 8 + 9)
                sp.dma_start(out[bass.ds(b, 1), :, :].rearrange("o c n -> (o c) n"), T2[0:CH, :]).then_inc(s_out, 16)
            sp.wait_ge(s_out, 16 * IMAGES + 16)

        @block.gpsimd
        def _(pl):
            nc.gpsimd.memset(w_p0[:], 0.0).then_inc(s_i0, 1)
            nc.gpsimd.memset(bias[:], 0.0).then_inc(s_i0, 1)
            nc.gpsimd.memset(x_w[:], 0.0).then_inc(s_i1, 1)
            nc.gpsimd.memset(kmask[:], 0.0).then_inc(s_i1, 1)
            nc.gpsimd.memset(VB[:], 0.0).then_inc(s_i1, 1)
            nc.gpsimd.memset(z_w[:, TOKENS:PADTOK], 0.0).then_inc(s_i1, 1)
            nc.gpsimd.memset(T4[:, TOKENS:PADTOK], 0.0).then_inc(s_i1, 1)
            nc.gpsimd.memset(QS[:], 0.0).then_inc(s_i1, 1)
            nc.gpsimd.memset(KS[:], 0.0).then_inc(s_i1, 1)
            pl.wait_ge(s_i1, 7)
            nc.gpsimd.memset(KS[STACK:STACK + SHIFT, :, 0:TOKENS], 1.0).then_inc(s_i1, 1)
            pl.wait_ge(s_i1, 8)
            nc.gpsimd.memset(minus_half, -0.5).then_inc(s_i1, 1)

            def reorder(n):
                for g in range(GROUPS):
                    src = x_in[:, g * GTOK:(g + 1) * GTOK].rearrange("c (i w j) -> c w i j", i=WIN, j=WIN)
                    dst = x_w[:, g * GTOK:(g + 1) * GTOK].rearrange("c (w i j) -> c w i j", i=WIN, j=WIN)
                    nc.gpsimd.tensor_copy(dst, src).then_inc(s_xw, 1)

            pl.wait_ge(s_xin, 16)
            reorder(0)
            with pl.Fori(0, IMAGES) as b:
                wait_apart(pl, s_xw, b * 8 + 8)
                for g in range(GROUPS):
                    if g >= 2:
                        wait_apart(pl, s_V, b * 8 + g - 1)
                    src = x_w[:, g * GTOK:(g + 1) * GTOK].rearrange("c (w m) -> c w m", m=WTOK)
                    nc.gpsimd.tensor_copy(x_tw[:, g % 2, :, :, :], src.unsqueeze(2).broadcast_to([CH, 8, 2, WTOK]))\
                      .then_inc(s_x2, 1)
                for i in range(3):
                    pl.wait_ge(s_pq, b * 3 + i + 1)
                    nc.gpsimd.tensor_tensor(gp[:, 0:1], gt[:, 0:1], minus_half[0:CH, :], ALU.pow).then_inc(s_pw, 1)
                wait_apart(pl, s_PV, b * 8 + 8)
                nc.gpsimd.memset(v_all[:, :, :, D1:32], 1.0).then_inc(s_ones, 1)
                wait_apart(pl, s_ones, b * 2 + 1)
                nc.gpsimd.memset(v_all[TOKENS % 128:128, :, TILES - 1, D1:32], 0.0).then_inc(s_ones, 1)
                pl.wait_ge(s_xin, b * 16 + 32)
                wait_apart(pl, s_h1, b * 8 + 8)
                reorder(b + 1)
                with pl.Fori(0, H1) as h:
                    hd = b * H1 + h
                    pl.wait_ge(s_va, b * 2 + 2)
                    pl.wait_ge(s_ones, b * 2 + 2)
                    wait_apart(pl, s_mx, hd * MAX_UNITS + 1)
                    nc.gpsimd.tensor_copy(v_h.rearrange("p t c -> p (t c)"),
                                          v_all_flat[:, bass.ds(h * TILES * 32, TILES * 32)]).then_inc(s_vh, 1)

        @block.scalar
        def _(act):
            def pair(t, c):
                return t[:, c * PAIR:(c + 1) * PAIR].rearrange("p (a n) -> p a n", a=2)

            HALF = TOKENS // 2
            act.wait_ge(s_i5, 1)
            nc.scalar.activation(qkscale[CH:128, :], scale_raw[CH:128, :], ACT.Exp).then_inc(s_i6, 1)
            act.wait_ge(s_w, 16 * NLOAD)
            with act.Fori(0, IMAGES) as b:
                act.wait_ge(s_out, b * 16 + 16)
                for c in range(4):
                    act.wait_ge(s_qk, b * 4 + c + 1)
                    src = PS[:, 2 * c:2 * c + 2, 0:GTOK]
                    nc.scalar.activation(pair(T2, c), src, ACT.Identity, bias=bqk0).then_inc(s_sq, 1)
                    nc.scalar.activation(pair(T3, c), src, ACT.Square, bias=bqk0).then_inc(s_sq, 1)
                for c in range(4):
                    act.wait_ge(s_max, b * 4 + c + 1)
                    nc.scalar.activation(pair(T3, c), pair(T3, c), ACT.Sqrt).then_inc(s_root, 1)
                for g in range(GROUPS + 1):
                    if g < GROUPS:
                        act.wait_ge(s_sub, b * 8 + g + 1)
                        nc.scalar.activation(Sb[:, g % 2, :], Sb[:, g % 2, :], ACT.Exp).then_inc(s_exp0, 1)
                    if g >= 1:
                        k = g - 1
                        for half in range(2):
                            act.wait_ge(s_T, b * 16 + 2 * k + half + 1)
                            if k >= 2:
                                act.wait_ge(s_PV, b * 8 + k - 1)
                            nc.scalar.activation(PT[0:2 * WTOK, k % 2, 2 * half:2 * half + 2, :],
                                                 PS[0:2 * WTOK, 4:6, :], ACT.Copy).then_inc(s_PT, 1)
                        act.wait_ge(s_PV, b * 8 + k + 1)
                        nc.scalar.activation(T2[:, k * GTOK:(k + 1) * GTOK], PS[:, 7, 0:GTOK], ACT.Copy)\
                          .then_inc(s_at, 1)
                for src, dst, fn, s, i in ((T3, T3, ACT.Relu, s_h, 0), (T3, T2, ACT.Identity, s_mi, 1)):
                    act.wait_ge(s_af, b * 3 + i + 1)
                    for a in range(2):
                        nc.scalar.activation(dst[0:CH, a * HALF:(a + 1) * HALF], src[0:CH, a * HALF:(a + 1) * HALF],
                                             fn, bias=gB[:, 0:1], scale=gA[:, 0:1]).then_inc(s, 1)
                for c in range(GROUPS):
                    act.wait_ge(s_m1, b * 8 + c + 1)
                    if c >= 2:
                        act.wait_ge(s_m2, b * 8 + c - 1)
                    for e in range(2):
                        nc.scalar.activation(hid[:, 2 * (c % 2) + e, 0:GTOK], PS[:, 2 * (c % 2) + e, 0:GTOK],
                                             ACT.Relu, bias=b1c[e]).then_inc(s_hid, 1)
                act.wait_ge(s_af, b * 3 + 3)
                for a in range(2):
                    nc.scalar.activation(z_w[:, a * HALF:(a + 1) * HALF], T3[0:CH, a * HALF:(a + 1) * HALF],
                                         ACT.Relu, bias=gB[:, 0:1], scale=gA[:, 0:1]).then_inc(s_z, 1)
                for c in range(5):
                    if c < 4:
                        act.wait_ge(s_gqk, b * 4 + c + 1)
                        nc.scalar.activation(pair(pieces[0], c), PS[:, 2 * c:2 * c + 2, 0:GTOK], ACT.Copy)\
                          .then_inc(s_ph, 1)
                    if c >= 1:
                        act.wait_ge(s_r, b * 4 + c)
                        nc.scalar.activation(pair(pieces[1], c - 1), pair(T3, c - 1), ACT.Copy).then_inc(s_pm, 1)
                with act.Fori(0, H1) as h:
                    hd = b * H1 + h
                    for u in range(EXP_UNITS):
                        act.wait_ge(s_gs, hd * EXP_UNITS + u + 1)
                        if u >= 4:
                            act.wait_ge(s_gpv, hd * EXP_UNITS + u - 3)
                        nc.scalar.activation(E[:, u % 4, :].rearrange("p (a n) -> p a n", a=2),
                                             PS[:, 2 * (u % 3):2 * (u % 3) + 2, 0:GTOK], ACT.Exp,
                                             scale=D1 ** -0.5).then_inc(s_ex, 1)

        @block.vector
        def _(dve):
            def pair(t, c):
                return t[:, c * PAIR:(c + 1) * PAIR].rearrange("p (a n) -> p a n", a=2)

            dve.wait_ge(s_w, 16 * NLOAD)
            dve.wait_ge(s_k, 16 * H0)
            nc.vector.tensor_scalar(scale_raw[CH:128, :], scale_raw[CH:128, :], LN100, None, ALU.min).then_inc(s_i5, 1)
            nc.vector.memset(qkscale[0:CH, :], 1.0).then_inc(s_setup, 1)
            nc.vector.tensor_copy(idb[:], idf[:]).then_inc(s_setup, 1)
            rel = T3[:, 0:WTOK * WTOK].bitcast(i32)
            hot = [T2[:, 0:WTOK * WTOK], SP_[:, :, :].rearrange("p a n -> p (a n)")[:, 0:WTOK * WTOK]]
            for r in range(2):
                nc.vector.tensor_scalar(hot[r], rel, rows_c[:, r:r + 1], None, ALU.is_equal).then_inc(s_i2, 1)
            NB = WTOK * WTOK // 7
            for c in range(7):
                dve.wait_ge(s_i3, c + 1)
                nc.vector.tensor_copy(T4[0:H0, c * NB:(c + 1) * NB], PS[0:H0, c, 0:NB]).then_inc(s_i4, 1)
            dve.wait_ge(s_i3, 8)
            nc.vector.tensor_tensor(pbias, PS[0:CH, 7, 0:1], pb0, ALU.add).then_inc(s_fin, 1)
            dve.wait_ge(s_setup, 2)
            dve.wait_ge(s_fin, 1)
            dve.wait_ge(s_i6, 1)
            dve.wait_ge(s_i1, 9)
            dve.wait_ge(s_bl, 16)
            dve.wait_ge(s_out, 16)

            with dve.Fori(0, IMAGES) as b:
                n = [0]

                def link(ins):
                    n[0] += 1
                    ins.then_inc(s_cd, 1)
                    dve.wait_ge(s_cd, b * CD + n[0])

                for c in range(4):
                    dve.wait_ge(s_ssq, b * 4 + c + 1)
                    nc.vector.tensor_scalar(pair(T3, c), PS[:, 2 * c:2 * c + 2, 0:GTOK], 1e-24, None, ALU.max)\
                      .then_inc(s_max, 1)
                for c in range(4):
                    dve.wait_ge(s_root, b * 4 + c + 1)
                    sl = slice(c * PAIR, (c + 1) * PAIR)
                    link(nc.vector.reciprocal(T3[:, sl], T3[:, sl]))
                    nc.vector.scalar_tensor_tensor(out=T4[:, sl], in0=T2[:, sl], scalar=qkscale, in1=T3[:, sl],
                                                   op0=ALU.mult, op1=ALU.mult).then_inc(s_qn, 1)

                def shift(g):
                    S = Sb[:, g % 2, :]
                    S3 = S.rearrange("p (a m) -> p a m", m=WTOK)
                    dve.wait_ge(s_S, b * 8 + g + 1)
                    if g >= 2:
                        dve.wait_ge(s_T, b * 16 + 2 * (g - 1))
                    nc.vector.tensor_tensor(S.rearrange("p (a n) -> p a n", a=4), PS[:, 0:4, 0:GTOK],
                                            bias[:].unsqueeze(1).broadcast_to([128, 4, GTOK]), ALU.add)\
                      .then_inc(s_add, 1)
                    dve.wait_ge(s_add, b * 8 + g + 1)
                    link(nc.vector.tensor_reduce(nmx, S3, op=ALU.max, axis=AX.X, negate=True))
                    nc.vector.tensor_tensor(S3, S3, nmx.unsqueeze(2).broadcast_to([128, 32, WTOK]), ALU.add)\
                      .then_inc(s_sub, 1)

                def v_blocks(g):
                    dve.wait_ge(s_V, b * 8 + g + 1)
                    if g >= 2:
                        dve.wait_ge(s_PV, b * 8 + g - 1)
                    nc.vector.tensor_tensor(VB[:, g % 2, :, :, 0:2 * D0].rearrange("p w q c -> p (w q) c"),
                                            PS[0:2 * WTOK, 6, :].rearrange("p (a c) -> p a c", c=2 * D0),
                                            vmask[:].unsqueeze(1).broadcast_to([2 * WTOK, 32, 2 * D0]), ALU.mult)\
                      .then_inc(s_vb, 1)

                def normalise(g):
                    S3 = Sb[:, g % 2, :].rearrange("p (a m) -> p a m", m=WTOK)
                    dve.wait_ge(s_exp0, b * 8 + g + 1)
                    link(nc.vector.reduce_sum(den, S3, axis=AX.X))
                    link(nc.vector.reciprocal(rden, den))
                    nc.vector.tensor_tensor(S3, S3, rden.unsqueeze(2).broadcast_to([128, 32, WTOK]), ALU.mult)\
                      .then_inc(s_P, 1)

                def residual(g):
                    sl = slice(g * GTOK, (g + 1) * GTOK)
                    dve.wait_ge(s_pr, b * 8 + g + 1)
                    nc.vector.scalar_tensor_tensor(out=T3[0:CH, sl], in0=PS[0:CH, 7, 0:GTOK], scalar=pbias,
                                                   in1=x_w[:, sl], op0=ALU.add, op1=ALU.add).then_inc(s_h1, 1)

                for g in range(GROUPS + 2):
                    if g < GROUPS:
                        shift(g)
                        v_blocks(g)
                    if 1 <= g <= GROUPS:
                        normalise(g - 1)
                    if g >= 2:
                        residual(g - 2)

                def group_norm(i):
                    for c in range(8):
                        last = nc.vector.bn_stats(stats[:, c, :], T3[0:CH, c * GTOK:(c + 1) * GTOK])
                        n[0] += 1
                        last.then_inc(s_cd, 1)
                    wait_apart(dve, s_cd, b * CD + n[0])
                    nc.vector.bn_aggr(mv, stats.rearrange("p c s -> p (c s)")).then_inc(s_gq, 1)
                    dve.wait_ge(s_gq, b * 6 + 2 * i + 1)
                    dve.wait_ge(s_gr, b * 6 + 2 * i + 1)
                    link(nc.vector.tensor_copy(gd[:, 1:2], PS[0:CH, 6, 0:1]))
                    link(nc.vector.tensor_tensor(gd[:, 0:1], mv[:, 0:1], gd[:, 1:2], ALU.subtract))
                    nc.vector.scalar_tensor_tensor(out=ge[:, 0:1], in0=gd[:, 0:1], scalar=gd[:, 0:1],
                                                   in1=mv[:, 1:2], op0=ALU.mult, op1=ALU.add).then_inc(s_gq, 1)
                    dve.wait_ge(s_gr, b * 6 + 2 * i + 2)
                    nc.vector.tensor_scalar(gt[:, 0:1], PS[0:CH, 6, 0:1], 1e-5, None, ALU.add).then_inc(s_pq, 1)
                    dve.wait_ge(s_pw, b * 3 + i + 1)
                    link(nc.vector.tensor_tensor(gA[:, 0:1], gp[:, 0:1], gn_w[i], ALU.mult))
                    link(nc.vector.tensor_tensor(ge[:, 1:2], gd[:, 1:2], gA[:, 0:1], ALU.mult))
                    nc.vector.tensor_tensor(gB[:, 0:1], gn_b[i], ge[:, 1:2], ALU.subtract).then_inc(s_af, 1)

                dve.wait_ge(s_h1, b * 8 + 8)
                group_norm(0)
                dve.wait_ge(s_h, b * 2 + 2)
                group_norm(1)
                for c in range(8):
                    sl = slice(c * GTOK, (c + 1) * GTOK)
                    dve.wait_ge(s_m2, b * 8 + c + 1)
                    nc.vector.scalar_tensor_tensor(out=T3[0:CH, sl], in0=PS[0:CH, 4 + c % 2, 0:GTOK], scalar=b2c,
                                                   in1=T3[0:CH, sl], op0=ALU.add, op1=ALU.add).then_inc(s_h2, 1)
                dve.wait_ge(s_h2, b * 8 + 8)
                group_norm(2)
                assert n[0] == CD, n[0]

                for c in range(5):
                    if c < 4:
                        dve.wait_ge(s_ph, b * 4 + c + 1)
                        nc.vector.tensor_tensor(pair(T3, c), PS[:, 2 * c:2 * c + 2, 0:GTOK], pair(pieces[0], c),
                                                ALU.subtract).then_inc(s_r, 1)
                    if c >= 1:
                        sl = slice((c - 1) * PAIR, c * PAIR)
                        dve.wait_ge(s_pm, b * 4 + c)
                        nc.vector.tensor_tensor(pieces[2][:, sl], T3[:, sl], pieces[1][:, sl], ALU.subtract)\
                          .then_inc(s_pl, 1)
                for k, (t0, t1) in enumerate(((0, 16), (16, TILES))):
                    dve.wait_ge(s_gv, b * 2 + k + 1)
                    nc.vector.tensor_copy(
                        v_all[:, :, t0:t1, 0:D1].rearrange("p h t c -> p t h c"),
                        PS[:, 2 * k:2 * k + 2, :].rearrange("p a n -> p (a n)")[:, 0:(t1 - t0) * CH]
                        .rearrange("p (t h c) -> p t h c", h=H1, c=D1)).then_inc(s_va, 1)

                with dve.Fori(0, H1) as h:
                    hd = b * H1 + h
                    for u in range(MAX_UNITS):
                        dve.wait_ge(s_mx, hd * MAX_UNITS + u + 1)
                        nc.vector.tensor_reduce(mxp[:, u:u + 1], PS[:, 2 * (u % 3):2 * (u % 3) + 2, 0:GTOK],
                                                op=ALU.max, axis=AX.XY).then_inc(s_mu, 1)
                    m = [0]

                    def step(ins):
                        m[0] += 1
                        ins.then_inc(s_ch, 1)
                        dve.wait_ge(s_ch, hd * 5 + m[0])

                    dve.wait_ge(s_mu, hd * MAX_UNITS + MAX_UNITS)
                    step(nc.vector.tensor_reduce(nm, mxp.rearrange("p (t q) -> p t q", q=4), op=ALU.max, axis=AX.X,
                                                 negate=True))
                    step(nc.vector.tensor_copy(nmp[:, 0, :], nm))
                    step(nc.vector.tensor_tensor(nr, nm, nmp[:, 0, :], ALU.subtract))
                    step(nc.vector.tensor_copy(nmp[:, 1, :], nr))
                    step(nc.vector.tensor_tensor(nr, nr, nmp[:, 1, :], ALU.subtract))
                    nc.vector.tensor_copy(nmp[:, 2, :], nr).then_inc(s_nm, 1)
                    dve.wait_ge(s_nt, hd + 1)
                    nc.vector.tensor_copy(nmt[:], PS[0:3 * TILES, 6, 0:64].bitcast(bf16)).then_inc(s_nc, 1)
                    for half in range(2):
                        dve.wait_ge(s_gpv, hd * EXP_UNITS + (half + 1) * EXP_UNITS // 2)
                        dve.wait_ge(s_st, b * 768 + 768)
                        nc.vector.tensor_copy(o_st[:, half, :], PS[:, 6 + half, 0:GTOK]).then_inc(s_o, 1)

                dve.wait_ge(s_dl, b * 16 + 16)
                nc.vector.reciprocal(rdcomp, dcomp).then_inc(s_dr, 1)
                dve.wait_ge(s_al, b * 16 + 16)
                dve.wait_ge(s_rl, b * 64 + 64)
                for c in range(4):
                    sl = slice(c * PAIR, (c + 1) * PAIR)
                    nc.vector.tensor_tensor(T4[0:CH, sl], T4[0:CH, sl], T3[0:CH, sl], ALU.mult).then_inc(s_ao, 1)
                for g in range(GROUPS):
                    sl = slice(g * GTOK, (g + 1) * GTOK)
                    dve.wait_ge(s_fp, b * 8 + g + 1)
                    nc.vector.tensor_tensor(T2[0:CH, sl].rearrange("c (i w j) -> c w i j", i=WIN, j=WIN),
                                            PS[0:CH, g, 0:GTOK].rearrange("c (w i j) -> c w i j", i=WIN, j=WIN),
                                            z_w[:, sl].rearrange("c (w i j) -> c w i j", i=WIN, j=WIN),
                                            ALU.add).then_inc(s_fin, 1)

        @block.tensor
        def _(pe):
            mm = nc.tensor.matmul
            pe.wait_ge(s_w, 16 * NLOAD)
            pe.wait_ge(s_i2, 2)
            hot = [T2[:, 0:WTOK * WTOK], SP_[:, :, :].rearrange("p a n -> p (a n)")[:, 0:WTOK * WTOK]]
            NB = WTOK * WTOK // 7
            for c in range(7):
                sl = slice(c * NB, (c + 1) * NB)
                mm(PS[0:H0, c, 0:NB], tab[:, 0, :], hot[0][:, sl], start=True, stop=False)
                mm(PS[0:H0, c, 0:NB], tab[0:TABLE - 128, 1, :], hot[1][0:TABLE - 128, sl], start=False, stop=True)\
                    .then_inc(s_i3, 1)
            mm(PS[0:CH, 7, 0:1], w_p0c[:], bv0, start=True, stop=True).then_inc(s_i3, 1)
            pe.wait_ge(s_setup, 2)
            pe.wait_ge(s_i4, 7)
            pe.wait_ge(s_i1, 9)

            with pe.Fori(0, IMAGES) as b:
                pe.wait_ge(s_fin, b * 8 + 1)
                for c in range(4):
                    pe.wait_ge(s_xw, b * 8 + 2 * c + 2)
                    for i in range(2):
                        g = 2 * c + i
                        last = mm(PS[:, g, 0:GTOK], w_qk0[:], x_w[:, g * GTOK:(g + 1) * GTOK], start=True, stop=True)
                    last.then_inc(s_qk, 1)
                for c in range(4):
                    pe.wait_ge(s_sq, b * 8 + 2 * c + 2)
                    for i in range(2):
                        g = 2 * c + i
                        last = mm(PS[:, g, 0:GTOK], hsum[:], T3[:, g * GTOK:(g + 1) * GTOK], start=True, stop=True)
                    last.then_inc(s_ssq, 1)

                def scores(g):
                    pe.wait_ge(s_km[g % 2], b * 512 + (g // 2 + 1) * 128)
                    if g == 0:
                        wait_apart(pe, s_qn, b * 4 + 4)
                    else:
                        wait_apart(pe, s_add, b * 8 + g)
                    for w in range(8):
                        q0 = g * GTOK + w * WTOK
                        last = mm(PS[64 * (w % 2):64 * (w % 2) + 64, w // 2, 0:GTOK], T4[0:CH, q0:q0 + 64],
                                  kmask[:, g % 2, :, w * WTOK:(w + 1) * WTOK], start=True, stop=True)
                    last.then_inc(s_S, 1)

                def values(g):
                    if g >= 1:
                        pe.wait_ge(s_vb, b * 8 + g)
                    pe.wait_ge(s_x2, b * 8 + g + 1)
                    for w in range(8):
                        last = mm(PS[0:2 * WTOK, 6, w * CH:(w + 1) * CH],
                                  x_tw[:, g % 2, w, :, :].rearrange("c a m -> c (a m)"), w_v0[:],
                                  start=True, stop=True)
                    last.then_inc(s_V, 1)

                def transpose(g):
                    pe.wait_ge(s_P, b * 8 + g + 1)
                    for half in range(2):
                        if 2 * g + half >= 1:
                            pe.wait_ge(s_PT, b * 16 + 2 * g + half)
                        for p in range(2):
                            for q in range(4):
                                c0 = (2 * half + p) * GTOK + q * 2 * WTOK
                                last = nc.tensor.transpose(PS[0:2 * WTOK, 4 + p, q * 128:(q + 1) * 128],
                                                           Sb[:, g % 2, c0:c0 + 2 * WTOK], idf[:])
                        last.then_inc(s_T, 1)

                def attend(g):
                    pe.wait_ge(s_PT, b * 16 + 2 * g + 2)
                    pe.wait_ge(s_vb, b * 8 + g + 1)
                    if g >= 1:
                        pe.wait_ge(s_h1, b * 8 + g)
                    for w in range(8):
                        for q in range(4):
                            c0 = q * 128 + 64 * (w % 2)
                            last = mm(PS[32 * q:32 * q + 32, 7, w * WTOK:(w + 1) * WTOK], VB[:, g % 2, w, q, :],
                                      PT[0:2 * WTOK, g % 2, w // 2, c0:c0 + WTOK], start=True, stop=True)
                    last.then_inc(s_PV, 1)
                    pe.wait_ge(s_at, b * 8 + g + 1)
                    mm(PS[0:CH, 7, 0:GTOK], w_p0[:], T2[:, g * GTOK:(g + 1) * GTOK], start=True, stop=True)\
                        .then_inc(s_pr, 1)

                for g in range(GROUPS + 1):
                    if g < GROUPS:
                        scores(g)
                        values(g)
                    if g >= 1:
                        transpose(g - 1)
                        attend(g - 1)

                def group_mean_of(i):
                    wait_apart(pe, s_gq, b * 6 + 2 * i + 1)
                    mm(PS[0:CH, 6, 0:1], gmean[:], mv[:, 0:1], start=True, stop=True).then_inc(s_gr, 1)
                    wait_apart(pe, s_gq, b * 6 + 2 * i + 2)
                    mm(PS[0:CH, 6, 0:1], gmean[:], ge[:, 0:1], start=True, stop=True).then_inc(s_gr, 1)

                group_mean_of(0)
                group_mean_of(1)
                for c in range(9):
                    if c < 8:
                        pe.wait_ge(s_mi, b * 2 + c // 4 + 1)
                        if c >= 2:
                            pe.wait_ge(s_hid, b * 16 + 2 * c - 2)
                        for e in range(2):
                            last = mm(PS[:, 2 * (c % 2) + e, 0:GTOK], w_1[:, 128 * e:128 * e + 128],
                                      T2[0:CH, c * GTOK:(c + 1) * GTOK], start=True, stop=True)
                        last.then_inc(s_m1, 1)
                    if c >= 1:
                        k = c - 1
                        pe.wait_ge(s_hid, b * 16 + 2 * c)
                        if k >= 2:
                            pe.wait_ge(s_h2, b * 8 + k - 1)
                        for e in range(2):
                            last = mm(PS[0:CH, 4 + k % 2, 0:GTOK], w_2[:, e, :], hid[:, 2 * (k % 2) + e, 0:GTOK],
                                      start=(e == 0), stop=(e == 1))
                        last.then_inc(s_m2, 1)
                group_mean_of(2)

                pe.wait_ge(s_z, b * 2 + 2)
                for c in range(4):
                    for i in range(2):
                        g = 2 * c + i
                        last = mm(PS[:, g, 0:GTOK], w_qk1[:], z_w[:, g * GTOK:(g + 1) * GTOK], start=True, stop=True)
                    last.then_inc(s_gqk, 1)
                for t in range(TILES):
                    if t % 16 == 0:
                        pe.wait_ge(s_r, b * 4 + t // 16 + 1)
                    last = mm(PS[:, t // 8, (t % 8) * CH:(t % 8 + 1) * CH], z_w[:, t * 128:(t + 1) * 128], w_v1[:],
                              start=True, stop=True)
                    if t in (15, TILES - 1):
                        last.then_inc(s_gv, 1)

                with pe.Fori(0, H1) as h:
                    hd = b * H1 + h
                    pe.wait_ge(s_st, b * 768 + 768)
                    pe.wait_ge(s_r, b * 4 + 4)
                    pe.wait_ge(s_va, b * 2 + 2)
                    for u in range(MAX_UNITS):
                        if u >= 3:
                            pe.wait_ge(s_mu, hd * MAX_UNITS + u - 2)
                        for i in range(2):
                            last = mm(PS[:, 2 * (u % 3) + i, 0:GTOK],
                                      QF[0:STACK, bass.ds(h * PADTOK + (u // 4) * 128, 128)],
                                      KF[0:STACK, bass.ds(h * PADTOK + (u % 4) * PAIR + i * GTOK, GTOK)],
                                      start=True, stop=True)
                        last.then_inc(s_mx, 1)
                    pe.wait_ge(s_nm, hd + 1)
                    nc.tensor.transpose(PS[0:3 * TILES, 6, 0:64].bitcast(bf16),
                                        nmp[:, :, :].rearrange("p c t -> p (c t)"), idb[:]).then_inc(s_nt, 1)
                    pe.wait_ge(s_sh, hd * 48 + 48)
                    pe.wait_ge(s_vh, hd + 1)
                    for u in range(EXP_UNITS + 2):
                        if u < EXP_UNITS:
                            if u >= 3:
                                pe.wait_ge(s_ex, hd * EXP_UNITS + u - 2)
                            half, kt, i = u // (2 * TILES), (u // 2) % TILES, u % 2
                            for j in range(2):
                                last = mm(PS[:, 2 * (u % 3) + j, 0:GTOK],
                                          KF[0:STACK + SHIFT, bass.ds(h * PADTOK + kt * 128, 128)],
                                          QF[0:STACK + SHIFT, bass.ds(h * PADTOK + (2 * half + i) * PAIR + j * GTOK,
                                                                      GTOK)], start=True, stop=True)
                            last.then_inc(s_gs, 1)
                        if u >= 2:
                            k = u - 2
                            half, kt, i = k // (2 * TILES), (k // 2) % TILES, k % 2
                            pe.wait_ge(s_ex, hd * EXP_UNITS + k + 1)
                            for j in range(2):
                                q0 = 32 * (2 * i + j)
                                last = mm(PS[q0:q0 + 32, 6 + half, 0:GTOK], v_h[:, kt, :],
                                          E[:, k % 4, j * GTOK:(j + 1) * GTOK], start=(kt == 0), stop=(kt == TILES - 1))
                            last.then_inc(s_gpv, 1)

                for g in range(GROUPS):
                    wait_apart(pe, s_ao, b * 4 + g // 2 + 1)
                    mm(PS[0:CH, g, 0:GTOK], w_p1[:], T4[0:CH, g * GTOK:(g + 1) * GTOK], start=True, stop=True)\
                        .then_inc(s_fp, 1)


def constants():
    import numpy as np

    head = np.arange(128) // D0
    group = np.arange(CH) // 4
    mask = np.repeat(np.arange(2), WTOK)[:, None] == np.repeat(np.arange(2), D0)[None, :]
    return {
        "ident": np.eye(128, dtype=np.float32),
        "head_sum": (head[:, None] == head[None, :]).astype(np.float32),
        "group_mean": (group[:, None] == group[None, :]).astype(np.float32) / 4,
        "head_mask": mask.astype(np.float32),
        "rows": np.stack([np.arange(128), np.arange(128) + 128], 1).astype(np.float32),
    }


_ORDER = ["x", "qkv_w", "qkv_b", "logit_scale", "bias_table", "rel_index", "proj_w", "proj_b", "gn1_w", "gn1_b",
          "gn2_w", "gn2_b", "mlp_gn_w", "mlp_gn_b", "mlp_w1", "mlp_b1", "mlp_w2", "mlp_b2"]
_TRANSPOSED = {"qkv_w", "proj_w", "mlp_w1", "mlp_w2"}


def kernel(**inputs):
    import numpy as np
    import concourse.bacc as bacc
    from concourse.bass_utils import run_bass_kernel_spmd as run

    given = {"x": np.asarray(inputs["x"]).reshape(IMAGES, CH, TOKENS)}
    for name in _ORDER[1:]:
        a = np.asarray(inputs["L0_conv_" + name])
        given[name] = a.T if name in _TRANSPOSED else a
    for name in ("w_qkv", "w_proj"):
        given[name] = np.asarray(inputs["L1_conv_" + name]).T
    given.update(constants())

    nc = bacc.Bacc("TRN2", target_bir_lowering=False, num_devices=1)
    arrays, args = {}, []
    for name, a in given.items():
        a = np.ascontiguousarray(a)
        arrays["in_" + name] = a
        args.append(nc.dram_tensor("in_" + name, a.shape, mybir.dt.from_np(a.dtype), kind="ExternalInput").ap())
    f32 = mybir.dt.float32
    args.append(nc.dram_tensor("out_0", [IMAGES, CH, TOKENS], f32, kind="ExternalOutput").ap())
    for name, shape in (("scratch_bias", [H0, WTOK * WTOK]), ("scratch_att", [CH, TOKENS]),
                        ("scratch_den", [H1, TOKENS]), ("scratch_rden", [H1, TOKENS])):
        args.append(nc.dram_tensor(name, shape, f32, kind="Internal").ap())
    nc.disable_value_cache = True
    attention_mlp_kernel(nc, *args)
    r = run(nc, [arrays], core_ids=[0])
    return r.results[0]["out_0"].reshape(IMAGES, CH, RES, RES)
```

```python
import concourse.bass as bass
from concourse import mybir
from contextlib import ExitStack

IMAGES, CH, RES, WIN = 16, 64, 56, 7
TOKENS = RES * RES
NWIN = (RES // WIN) ** 2
WTOK = WIN * WIN
GROUPS = RES // WIN
GTOK = TOKENS // GROUPS
H0, D0 = 8, 8
H1, D1 = 4, 16
HID = 256
TABLE = (2 * WIN - 1) ** 2
TILES = -(-TOKENS // 128)
PADTOK = TILES * 128
PAIR = 2 * GTOK
PIECES = 6
STACK = PIECES * D1
SHIFT = 3
MAX_HALF = 112
EXP_UNITS = 2 * TILES * 2
MAX_UNITS = TILES * GROUPS
LN100 = 4.605170185988092


def attention_mlp_kernel(nc, x, qkv0, qkv0_b, logit_scale, table, rel_index, proj0, proj0_b, gn1_w, gn1_b,
                         gn2_w, gn2_b, gnm_w, gnm_b, w1, b1, w2, b2, qkv1, proj1,
                         ident, head_sum, group_mean, head_mask, rows, out, scratch_bias, scratch_att, scratch_den,
                         scratch_rden):
    f32, bf16, i32 = mybir.dt.float32, mybir.dt.bfloat16, mybir.dt.int32
    ALU, ACT, AX = mybir.AluOpType, mybir.ActivationFunctionType, mybir.AxisListType

    ctx = ExitStack()
    with ctx:
        def sb(name, shape, dt=f32):
            return ctx.enter_context(nc.sbuf_tensor(name, shape, dt))

        def sem(name):
            return ctx.enter_context(nc.semaphore(name))

        w_qk0 = sb("w_qk0", [CH, 128])
        w_v0 = sb("w_v0", [CH, CH])
        w_p0 = sb("w_p0", [128, CH])
        w_p0c = sb("w_p0c", [CH, CH])
        w_1 = sb("w_1", [CH, HID])
        w_2 = sb("w_2", [128, 2, CH])
        w_qk1 = sb("w_qk1", [CH, 128])
        w_v1 = sb("w_v1", [CH, CH])
        w_p1 = sb("w_p1", [CH, CH])
        vec = sb("vec", [128, 24])
        bqk0, pb0, bv0, b2c = vec[:, 0:1], vec[0:CH, 1:2], vec[0:CH, 2:3], vec[0:CH, 3:4]
        b1c = [vec[:, 4:5], vec[:, 5:6]]
        gn_w = [vec[0:CH, 6 + 2 * i:7 + 2 * i] for i in range(3)]
        gn_b = [vec[0:CH, 7 + 2 * i:8 + 2 * i] for i in range(3)]
        qkscale, rows_c = vec[:, 12:13], vec[:, 13:15]
        scale_raw, minus_half = vec[:, 15:16], vec[:, 16:17]
        pbias = vec[0:CH, 17:18]
        idf = sb("idf", [128, 128])
        idb = sb("idb", [128, 128], bf16)
        hsum = sb("hsum", [128, 128])
        gmean = sb("gmean", [CH, CH])
        vmask = sb("vmask", [2 * WTOK, 2 * D0])
        tab = sb("tab", [128, 2, H0])
        bias = sb("bias", [128, H0 * WTOK])

        x_in = sb("x_in", [CH, TOKENS])
        x_w = sb("x_w", [CH, PADTOK])
        T2 = sb("T2", [128, TOKENS])
        T3 = sb("T3", [128, TOKENS])
        T4 = sb("T4", [128, PADTOK])
        z_w = sb("z_w", [CH, PADTOK])
        kmask = sb("kmask", [CH, 2, H0, GTOK])
        SP_ = sb("SPx", [128, 4, PAIR])
        PV_ = sb("PVx", [128, 2, 4, 512])
        VB = sb("VB", [2 * WTOK, 2, 8, 4, 32])
        piece_l = sb("piece_l", [128, TOKENS], bf16)
        pieces = [T2[:, :].bitcast(bf16)[:, 0:TOKENS], T2[:, :].bitcast(bf16)[:, TOKENS:2 * TOKENS], piece_l[:, :]]
        QS = sb("QS", [128, H1, PADTOK], bf16)
        KS = sb("KS", [128, H1, PADTOK], bf16)
        small = sb("small", [128, 256])
        nmt = sb("nmt", [3 * TILES, 128], bf16)
        nmp = sb("nmp", [128, 3, TILES], bf16)
        o_st = T2[:, 0:2 * GTOK].rearrange("p (a n) -> p a n", a=2)

        Sb = SP_[:, :, :].rearrange("p a n -> p (a n)").rearrange("p (b c n) -> p b c n", b=2, c=4)
        Sb = SP_[:, :, :].rearrange("p (b c) n -> p b (c n)", b=2)
        hid = SP_[:, :, :]
        E = SP_[:, :, :]
        PT = PV_
        v_all = PV_[:, :, :, :].rearrange("p a b n -> p (a b n)")[:, 0:H1 * TILES * 32]
        v_all = v_all.rearrange("p (h t c) -> p h t c", h=H1, t=TILES)
        x_tw = sb("x_tw", [CH, 2, 8, 2, WTOK])
        nmx, den, rden = small[:, 0:32], small[:, 32:64], small[:, 64:96]
        stats = small[0:CH, 96:144].rearrange("p (c s) -> p c s", c=8)
        mv, gd, ge, gt, gp, gA, gB = (small[0:CH, 144 + 4 * i:146 + 4 * i] for i in range(7))
        mxp = small[:, 0:MAX_UNITS]
        nm = small[:, 200:225]
        nr = small[:, 225:250]
        dcomp = small[:, 0:98]
        rdcomp = small[:, 98:196]

        PS = ctx.enter_context(nc.psum_tensor("PS", [128, 8, 512], f32))

        s_w, s_k = sem("weights_loaded"), sem("scale_loaded")
        s_i0, s_i1, s_i2, s_i3, s_i4, s_i5, s_i6 = (sem(f"setup{i}") for i in range(7))
        s_bd, s_bl = sem("bias_stored"), sem("bias_loaded")
        s_setup = sem("setup_chain")
        s_xin, s_xw, s_x2 = sem("x_loaded"), sem("x_by_windows"), sem("x_twice")
        s_qk, s_sq, s_ssq, s_max, s_root, s_qn = (sem(n) for n in (
            "qk_product", "qk_squares", "head_sums", "sums_bounded", "roots", "qk_normalised"))
        s_km = [sem("kmask_even"), sem("kmask_odd")]
        s_S, s_add, s_sub, s_exp0, s_P, s_V, s_vb = (sem(n) for n in (
            "win_scores", "win_biased", "win_shifted", "win_exps", "win_probs", "win_v", "win_v_blocks"))
        s_T, s_PT, s_PV, s_at, s_pr, s_h1 = (sem(n) for n in (
            "win_transposed", "win_transposed_copied", "win_pv", "win_att", "win_proj", "residual1"))
        s_gq, s_gr, s_pq, s_pw, s_af = (sem(n) for n in (
            "gn_request", "gn_mean", "pow_request", "pow_done", "gn_affine"))
        s_h, s_mi, s_m1, s_hid, s_m2, s_h2, s_z = (sem(n) for n in (
            "h_ready", "mlp_in", "mlp1", "hidden", "mlp2", "residual2", "z_ready"))
        s_gqk, s_ph, s_r, s_pm, s_pl, s_gv, s_va, s_ones = (sem(n) for n in (
            "gqk", "piece_h", "rest", "piece_m", "piece_l", "gv", "v_all_ready", "ones_set"))
        s_st = [sem(f"stacks_loaded{h}") for h in range(H1)]
        s_mx, s_mu, s_nm, s_nt, s_nc, s_sh = (sem(n) for n in (
            "max_scores", "max_taken", "max_pieces", "max_transposed", "max_copied", "shift_loaded"))
        s_vh, s_gs, s_ex, s_gpv, s_o, s_od = (sem(n) for n in (
            "v_head", "scores", "exps", "pv_done", "out_copied", "out_stored"))
        s_al, s_dl, s_dr, s_ds, s_rl, s_ao, s_fp, s_fin, s_out = (sem(n) for n in (
            "att_loaded", "den_loaded", "den_inverted", "rden_stored", "rden_loaded", "att_scaled",
            "final_proj", "final", "out_written"))
        s_cd, s_ch, s_cf = sem("dve_chain"), sem("dve_head_chain"), sem("dve_final_chain")
        CD = 64

        def wait_apart(eng, semaphore, value):
            value = eng.to_reg(value)
            eng.wait_ge(s_i1, 9)
            eng.wait_ge(semaphore, value)

        block = ctx.enter_context(nc.Block())
        NLOAD = 32

        @block.sync
        def _(sp):
            def load(dst, src, s=s_w):
                sp.dma_start(dst, src).then_inc(s, 16)

            col = lambda v: v.rearrange("(n o) -> n o", o=1)
            load(T3[:, 0:WTOK * WTOK].bitcast(i32), rel_index.rearrange("n m -> (n m)").partition_broadcast(128))
            load(tab[:, 0, :], table[0:128, :])
            load(tab[0:TABLE - 128, 1, :], table[128:TABLE, :])
            load(rows_c, rows)
            load(w_qk0[:], qkv0[:, 0:128])
            load(w_v0[:], qkv0[:, 128:192])
            sp.wait_ge(s_i0, 2)
            for p in range(4):
                load(w_p0[32 * p:32 * p + 16, :], proj0[16 * p:16 * p + 16, :])
            load(w_p0c[:], proj0)
            load(w_1[:], w1)
            load(w_2[:], w2.rearrange("(a p) c -> p a c", a=2))
            load(w_qk1[:], qkv1[:, 0:128])
            load(w_v1[:], qkv1[:, 128:192])
            load(w_p1[:], proj1)
            load(bqk0, col(qkv0_b[0:128]))
            load(bv0, col(qkv0_b[128:192]))
            load(pb0, col(proj0_b))
            load(b2c, col(b2))
            load(b1c[0], col(b1[0:128]))
            load(b1c[1], col(b1[128:256]))
            for i, (w_, b_) in enumerate(((gn1_w, gn1_b), (gnm_w, gnm_b), (gn2_w, gn2_b))):
                load(gn_w[i], col(w_))
                load(gn_b[i], col(b_))
            load(idf[:], ident)
            load(hsum[:], head_sum)
            load(gmean[:], group_mean)
            load(vmask[:], head_mask)
            for h in range(H0):
                load(scale_raw[CH + D0 * h:CH + D0 * h + D0, :],
                     logit_scale[h:h + 1].partition_broadcast(D0), s_k)
            sp.wait_ge(s_i4, 7)
            sp.dma_start(scratch_bias, T4[0:H0, 0:WTOK * WTOK]).then_inc(s_bd, 16)
            sp.wait_ge(s_bd, 16)
            sp.wait_ge(s_i0, 2)
            for q in range(2):
                sp.dma_start(bias[64 * q:64 * q + WTOK, :].rearrange("n (h m) -> n h m", h=H0),
                             scratch_bias.rearrange("h (n m) -> n h m", n=WTOK)).then_inc((s_bl, s_out)[q], 16)
            sp.dma_start(x_in[:], x[0, :, :]).then_inc(s_xin, 16)

            with sp.Fori(0, IMAGES) as b:
                sp.wait_ge(s_xw, b * 8 + 8)
                sp.dma_start(x_in[:], x[bass.ds((b + 1) % IMAGES, 1), :, :].rearrange("o c n -> (o c) n"))\
                  .then_inc(s_xin, 16)
                for g in range(GROUPS):
                    sp.wait_ge(s_qn, b * 4 + g // 2 + 1)
                    if g >= 2:
                        sp.wait_ge(s_S, b * 8 + g - 1)
                    for h in range(H0):
                        sp.dma_start(kmask[D0 * h:D0 * h + D0, g % 2, h, :],
                                     T4[CH + D0 * h:CH + D0 * h + D0, g * GTOK:(g + 1) * GTOK])\
                          .then_inc(s_km[g % 2], 16)
                sp.wait_ge(s_pl, b * 4 + 4)
                sp.wait_ge(s_pm, b * 4 + 4)
                for h in range(H1):
                    for dst, base, order in ((QS, 0, (0, 0, 1, 1, 0, 2)), (KS, CH, (0, 1, 0, 1, 2, 0))):
                        for j, pc in enumerate(order):
                            sp.dma_start(dst[D1 * j:D1 * j + D1, h, 0:TOKENS],
                                         pieces[pc][base + D1 * h:base + D1 * h + D1, :]).then_inc(s_st[h], 16)

                def shift_rows(h):
                    sp.wait_ge(s_nc, b * H1 + h + 1)
                    for pc in range(3):
                        sp.dma_start(QS[STACK + pc:STACK + pc + 1, h, :]
                                     .rearrange("p (t n) -> p t n", n=128),
                                     nmt[TILES * pc:TILES * pc + TILES, :]).then_inc(s_sh, 16)

                def store_half(h, half):
                    hd = b * H1 + h
                    sp.wait_ge(s_o, hd * 2 + half + 1)
                    for j in range(4):
                        c0 = (4 * half + j) * GTOK
                        sp.dma_start(scratch_att[h * D1:(h + 1) * D1, c0:c0 + GTOK],
                                     o_st[32 * j:32 * j + D1, half, :]).then_inc(s_od, 16)
                        sp.dma_start(scratch_den[h:h + 1, c0:c0 + GTOK],
                                     o_st[32 * j + D1:32 * j + D1 + 1, half, :]).then_inc(s_od, 16)
                    wait_apart(sp, s_od, hd * 256 + (half + 1) * 128)

                shift_rows(0)
                for h in range(H1 - 1):
                    store_half(h, 0)
                    shift_rows(h + 1)
                    store_half(h, 1)
                store_half(H1 - 1, 0)
                store_half(H1 - 1, 1)
                sp.dma_start(dcomp, scratch_den.rearrange("h (a n) -> (h a) n", a=32)).then_inc(s_dl, 16)
                sp.dma_start(T4[0:CH, 0:TOKENS], scratch_att).then_inc(s_al, 16)
                sp.wait_ge(s_dr, b + 1)
                sp.dma_start(scratch_rden.rearrange("h (a n) -> (h a) n", a=32), rdcomp).then_inc(s_ds, 16)
                sp.wait_ge(s_ds, b * 16 + 16)
                for h in range(H1):
                    sp.dma_start(T3[D1 * h:D1 * h + D1, 0:TOKENS], scratch_rden[h, :].partition_broadcast(D1))\
                      .then_inc(s_rl, 16)
                sp.wait_ge(s_fin, b * 8 + 9)
                sp.dma_start(out[bass.ds(b, 1), :, :].rearrange("o c n -> (o c) n"), T2[0:CH, :]).then_inc(s_out, 16)
            sp.wait_ge(s_out, 16 * IMAGES + 16)

        @block.gpsimd
        def _(pl):
            nc.gpsimd.memset(w_p0[:], 0.0).then_inc(s_i0, 1)
            nc.gpsimd.memset(bias[:], 0.0).then_inc(s_i0, 1)
            nc.gpsimd.memset(x_w[:], 0.0).then_inc(s_i1, 1)
            nc.gpsimd.memset(kmask[:], 0.0).then_inc(s_i1, 1)
            nc.gpsimd.memset(VB[:], 0.0).then_inc(s_i1, 1)
            nc.gpsimd.memset(z_w[:, TOKENS:PADTOK], 0.0).then_inc(s_i1, 1)
            nc.gpsimd.memset(T4[:, TOKENS:PADTOK], 0.0).then_inc(s_i1, 1)
            nc.gpsimd.memset(QS[:], 0.0).then_inc(s_i1, 1)
            nc.gpsimd.memset(KS[:], 0.0).then_inc(s_i1, 1)
            pl.wait_ge(s_i1, 7)
            nc.gpsimd.memset(KS[STACK:STACK + SHIFT, :, 0:TOKENS], 1.0).then_inc(s_i1, 1)
            pl.wait_ge(s_i1, 8)
            nc.gpsimd.memset(minus_half, -0.5).then_inc(s_i1, 1)

            def reorder(n):
                for g in range(GROUPS):
                    src = x_in[:, g * GTOK:(g + 1) * GTOK].rearrange("c (i w j) -> c w i j", i=WIN, j=WIN)
                    dst = x_w[:, g * GTOK:(g + 1) * GTOK].rearrange("c (w i j) -> c w i j", i=WIN, j=WIN)
                    nc.gpsimd.tensor_copy(dst, src).then_inc(s_xw, 1)

            pl.wait_ge(s_xin, 16)
            reorder(0)
            with pl.Fori(0, IMAGES) as b:
                wait_apart(pl, s_xw, b * 8 + 8)
                for g in range(GROUPS):
                    if g >= 2:
                        wait_apart(pl, s_V, b * 8 + g - 1)
                    src = x_w[:, g * GTOK:(g + 1) * GTOK].rearrange("c (w m) -> c w m", m=WTOK)
                    nc.gpsimd.tensor_copy(x_tw[:, g % 2, :, :, :], src.unsqueeze(2).broadcast_to([CH, 8, 2, WTOK]))\
                      .then_inc(s_x2, 1)
                for i in range(3):
                    pl.wait_ge(s_pq, b * 3 + i + 1)
                    nc.gpsimd.tensor_tensor(gp[:, 0:1], gt[:, 0:1], minus_half[0:CH, :], ALU.pow).then_inc(s_pw, 1)
                wait_apart(pl, s_PV, b * 8 + 8)
                nc.gpsimd.memset(v_all[:, :, :, D1:32], 1.0).then_inc(s_ones, 1)
                wait_apart(pl, s_ones, b * 2 + 1)
                nc.gpsimd.memset(v_all[TOKENS % 128:128, :, TILES - 1, D1:32], 0.0).then_inc(s_ones, 1)
                pl.wait_ge(s_xin, b * 16 + 32)
                wait_apart(pl, s_h1, b * 8 + 8)
                reorder(b + 1)

        @block.scalar
        def _(act):
            def pair(t, c):
                return t[:, c * PAIR:(c + 1) * PAIR].rearrange("p (a n) -> p a n", a=2)

            HALF = TOKENS // 2
            act.wait_ge(s_i5, 1)
            nc.scalar.activation(qkscale[CH:128, :], scale_raw[CH:128, :], ACT.Exp).then_inc(s_i6, 1)
            act.wait_ge(s_w, 16 * NLOAD)
            with act.Fori(0, IMAGES) as b:
                act.wait_ge(s_out, b * 16 + 16)
                for c in range(4):
                    act.wait_ge(s_qk, b * 4 + c + 1)
                    src = PS[:, 2 * c:2 * c + 2, 0:GTOK]
                    nc.scalar.activation(pair(T2, c), src, ACT.Identity, bias=bqk0).then_inc(s_sq, 1)
                    nc.scalar.activation(pair(T3, c), src, ACT.Square, bias=bqk0).then_inc(s_sq, 1)
                for c in range(4):
                    act.wait_ge(s_max, b * 4 + c + 1)
                    nc.scalar.activation(pair(T3, c), pair(T3, c), ACT.Sqrt).then_inc(s_root, 1)
                for g in range(GROUPS + 1):
                    if g < GROUPS:
                        act.wait_ge(s_sub, b * 8 + g + 1)
                        nc.scalar.activation(Sb[:, g % 2, :], Sb[:, g % 2, :], ACT.Exp).then_inc(s_exp0, 1)
                    if g >= 1:
                        k = g - 1
                        for half in range(2):
                            act.wait_ge(s_T, b * 16 + 2 * k + half + 1)
                            if k >= 2:
                                act.wait_ge(s_PV, b * 8 + k - 1)
                            nc.scalar.activation(PT[0:2 * WTOK, k % 2, 2 * half:2 * half + 2, :],
                                                 PS[0:2 * WTOK, 4:6, :], ACT.Copy).then_inc(s_PT, 1)
                        act.wait_ge(s_PV, b * 8 + k + 1)
                        nc.scalar.activation(T2[:, k * GTOK:(k + 1) * GTOK], PS[:, 7, 0:GTOK], ACT.Copy)\
                          .then_inc(s_at, 1)
                for src, dst, fn, s, i in ((T3, T3, ACT.Relu, s_h, 0), (T3, T2, ACT.Identity, s_mi, 1)):
                    act.wait_ge(s_af, b * 3 + i + 1)
                    for a in range(2):
                        nc.scalar.activation(dst[0:CH, a * HALF:(a + 1) * HALF], src[0:CH, a * HALF:(a + 1) * HALF],
                                             fn, bias=gB[:, 0:1], scale=gA[:, 0:1]).then_inc(s, 1)
                for c in range(GROUPS):
                    act.wait_ge(s_m1, b * 8 + c + 1)
                    if c >= 2:
                        act.wait_ge(s_m2, b * 8 + c - 1)
                    for e in range(2):
                        nc.scalar.activation(hid[:, 2 * (c % 2) + e, 0:GTOK], PS[:, 2 * (c % 2) + e, 0:GTOK],
                                             ACT.Relu, bias=b1c[e]).then_inc(s_hid, 1)
                act.wait_ge(s_af, b * 3 + 3)
                for a in range(2):
                    nc.scalar.activation(z_w[:, a * HALF:(a + 1) * HALF], T3[0:CH, a * HALF:(a + 1) * HALF],
                                         ACT.Relu, bias=gB[:, 0:1], scale=gA[:, 0:1]).then_inc(s_z, 1)
                for c in range(5):
                    if c < 4:
                        act.wait_ge(s_gqk, b * 4 + c + 1)
                        nc.scalar.activation(pair(pieces[0], c), PS[:, 2 * c:2 * c + 2, 0:GTOK], ACT.Copy)\
                          .then_inc(s_ph, 1)
                    if c >= 1:
                        act.wait_ge(s_r, b * 4 + c)
                        nc.scalar.activation(pair(pieces[1], c - 1), pair(T3, c - 1), ACT.Copy).then_inc(s_pm, 1)
                for h in range(H1):
                    hd = b * H1 + h
                    for u in range(EXP_UNITS):
                        act.wait_ge(s_gs, hd * EXP_UNITS + u + 1)
                        if u >= 4:
                            act.wait_ge(s_gpv, hd * EXP_UNITS + u - 3)
                        nc.scalar.activation(E[:, u % 4, :].rearrange("p (a n) -> p a n", a=2),
                                             PS[:, 2 * (u % 2):2 * (u % 2) + 2, 0:GTOK], ACT.Exp,
                                             scale=D1 ** -0.5).then_inc(s_ex, 1)

        @block.vector
        def _(dve):
            def pair(t, c):
                return t[:, c * PAIR:(c + 1) * PAIR].rearrange("p (a n) -> p a n", a=2)

            dve.wait_ge(s_w, 16 * NLOAD)
            dve.wait_ge(s_k, 16 * H0)
            nc.vector.tensor_scalar(scale_raw[CH:128, :], scale_raw[CH:128, :], LN100, None, ALU.min).then_inc(s_i5, 1)
            nc.vector.memset(qkscale[0:CH, :], 1.0).then_inc(s_setup, 1)
            nc.vector.tensor_copy(idb[:], idf[:]).then_inc(s_setup, 1)
            rel = T3[:, 0:WTOK * WTOK].bitcast(i32)
            hot = [T2[:, 0:WTOK * WTOK], SP_[:, :, :].rearrange("p a n -> p (a n)")[:, 0:WTOK * WTOK]]
            for r in range(2):
                nc.vector.tensor_scalar(hot[r], rel, rows_c[:, r:r + 1], None, ALU.is_equal).then_inc(s_i2, 1)
            NB = WTOK * WTOK // 7
            for c in range(7):
                dve.wait_ge(s_i3, c + 1)
                nc.vector.tensor_copy(T4[0:H0, c * NB:(c + 1) * NB], PS[0:H0, c, 0:NB]).then_inc(s_i4, 1)
            dve.wait_ge(s_i3, 8)
            nc.vector.tensor_tensor(pbias, PS[0:CH, 7, 0:1], pb0, ALU.add).then_inc(s_fin, 1)
            dve.wait_ge(s_setup, 2)
            dve.wait_ge(s_fin, 1)
            dve.wait_ge(s_i6, 1)
            dve.wait_ge(s_i1, 9)
            dve.wait_ge(s_bl, 16)
            dve.wait_ge(s_out, 16)

            with dve.Fori(0, IMAGES) as b:
                n = [0]

                def link(ins):
                    n[0] += 1
                    ins.then_inc(s_cd, 1)
                    dve.wait_ge(s_cd, b * CD + n[0])

                for c in range(4):
                    dve.wait_ge(s_ssq, b * 4 + c + 1)
                    nc.vector.tensor_scalar(pair(T3, c), PS[:, 2 * c:2 * c + 2, 0:GTOK], 1e-24, None, ALU.max)\
                      .then_inc(s_max, 1)

                def normalise_qk(c):
                    dve.wait_ge(s_root, b * 4 + c + 1)
                    sl = slice(c * PAIR, (c + 1) * PAIR)
                    link(nc.vector.reciprocal(T3[:, sl], T3[:, sl]))
                    nc.vector.scalar_tensor_tensor(out=T4[:, sl], in0=T2[:, sl], scalar=qkscale, in1=T3[:, sl],
                                                   op0=ALU.mult, op1=ALU.mult).then_inc(s_qn, 1)

                def shift(g):
                    S = Sb[:, g % 2, :]
                    S3 = S.rearrange("p (a m) -> p a m", m=WTOK)
                    dve.wait_ge(s_S, b * 8 + g + 1)
                    if g >= 2:
                        dve.wait_ge(s_T, b * 16 + 2 * (g - 1))
                    nc.vector.tensor_tensor(S.rearrange("p (a n) -> p a n", a=4), PS[:, 0:4, 0:GTOK],
                                            bias[:].unsqueeze(1).broadcast_to([128, 4, GTOK]), ALU.add)\
                      .then_inc(s_add, 1)
                    dve.wait_ge(s_add, b * 8 + g + 1)
                    link(nc.vector.tensor_reduce(nmx, S3, op=ALU.max, axis=AX.X, negate=True))
                    nc.vector.tensor_tensor(S3, S3, nmx.unsqueeze(2).broadcast_to([128, 32, WTOK]), ALU.add)\
                      .then_inc(s_sub, 1)

                def v_blocks(g):
                    dve.wait_ge(s_V, b * 8 + g + 1)
                    if g >= 2:
                        dve.wait_ge(s_PV, b * 8 + g - 1)
                    nc.vector.tensor_tensor(VB[:, g % 2, :, :, 0:2 * D0].rearrange("p w q c -> p (w q) c"),
                                            PS[0:2 * WTOK, 6, :].rearrange("p (a c) -> p a c", c=2 * D0),
                                            vmask[:].unsqueeze(1).broadcast_to([2 * WTOK, 32, 2 * D0]), ALU.mult)\
                      .then_inc(s_vb, 1)

                def normalise(g):
                    S3 = Sb[:, g % 2, :].rearrange("p (a m) -> p a m", m=WTOK)
                    dve.wait_ge(s_exp0, b * 8 + g + 1)
                    link(nc.vector.reduce_sum(den, S3, axis=AX.X))
                    link(nc.vector.reciprocal(rden, den))
                    nc.vector.tensor_tensor(S3, S3, rden.unsqueeze(2).broadcast_to([128, 32, WTOK]), ALU.mult)\
                      .then_inc(s_P, 1)

                def residual(g):
                    sl = slice(g * GTOK, (g + 1) * GTOK)
                    dve.wait_ge(s_pr, b * 8 + g + 1)
                    nc.vector.scalar_tensor_tensor(out=T3[0:CH, sl], in0=PS[0:CH, 7, 0:GTOK], scalar=pbias,
                                                   in1=x_w[:, sl], op0=ALU.add, op1=ALU.add).then_inc(s_h1, 1)

                normalise_qk(0)
                normalise_qk(1)
                for g in range(GROUPS + 2):
                    if 1 <= g <= GROUPS:
                        normalise(g - 1)
                    if g < GROUPS:
                        shift(g)
                        v_blocks(g)
                    if g < 2:
                        normalise_qk(g + 2)
                    else:
                        residual(g - 2)

                def group_norm(i):
                    for c in range(8):
                        last = nc.vector.bn_stats(stats[:, c, :], T3[0:CH, c * GTOK:(c + 1) * GTOK])
                        n[0] += 1
                        last.then_inc(s_cd, 1)
                    wait_apart(dve, s_cd, b * CD + n[0])
                    nc.vector.bn_aggr(mv, stats.rearrange("p c s -> p (c s)")).then_inc(s_gq, 1)
                    dve.wait_ge(s_gq, b * 6 + 2 * i + 1)
                    dve.wait_ge(s_gr, b * 6 + 2 * i + 1)
                    link(nc.vector.tensor_copy(gd[:, 1:2], PS[0:CH, 6, 0:1]))
                    link(nc.vector.tensor_tensor(gd[:, 0:1], mv[:, 0:1], gd[:, 1:2], ALU.subtract))
                    nc.vector.scalar_tensor_tensor(out=ge[:, 0:1], in0=gd[:, 0:1], scalar=gd[:, 0:1],
                                                   in1=mv[:, 1:2], op0=ALU.mult, op1=ALU.add).then_inc(s_gq, 1)
                    dve.wait_ge(s_gr, b * 6 + 2 * i + 2)
                    nc.vector.tensor_scalar(gt[:, 0:1], PS[0:CH, 6, 0:1], 1e-5, None, ALU.add).then_inc(s_pq, 1)
                    dve.wait_ge(s_pw, b * 3 + i + 1)
                    link(nc.vector.tensor_tensor(gA[:, 0:1], gp[:, 0:1], gn_w[i], ALU.mult))
                    link(nc.vector.tensor_tensor(ge[:, 1:2], gd[:, 1:2], gA[:, 0:1], ALU.mult))
                    nc.vector.tensor_tensor(gB[:, 0:1], gn_b[i], ge[:, 1:2], ALU.subtract).then_inc(s_af, 1)

                dve.wait_ge(s_h1, b * 8 + 8)
                group_norm(0)
                dve.wait_ge(s_h, b * 2 + 2)
                group_norm(1)
                for c in range(8):
                    sl = slice(c * GTOK, (c + 1) * GTOK)
                    dve.wait_ge(s_m2, b * 8 + c + 1)
                    nc.vector.scalar_tensor_tensor(out=T3[0:CH, sl], in0=PS[0:CH, 4 + c % 2, 0:GTOK], scalar=b2c,
                                                   in1=T3[0:CH, sl], op0=ALU.add, op1=ALU.add).then_inc(s_h2, 1)
                dve.wait_ge(s_h2, b * 8 + 8)
                group_norm(2)
                assert n[0] == CD, n[0]

                for c in range(5):
                    if c < 4:
                        dve.wait_ge(s_ph, b * 4 + c + 1)
                        nc.vector.tensor_tensor(pair(T3, c), PS[:, 2 * c:2 * c + 2, 0:GTOK], pair(pieces[0], c),
                                                ALU.subtract).then_inc(s_r, 1)
                    if c >= 1:
                        sl = slice((c - 1) * PAIR, c * PAIR)
                        dve.wait_ge(s_pm, b * 4 + c)
                        nc.vector.tensor_tensor(pieces[2][:, sl], T3[:, sl], pieces[1][:, sl], ALU.subtract)\
                          .then_inc(s_pl, 1)
                for k, (t0, t1) in enumerate(((0, 16), (16, TILES))):
                    dve.wait_ge(s_gv, b * 2 + k + 1)
                    nc.vector.tensor_copy(
                        v_all[:, :, t0:t1, 0:D1].rearrange("p h t c -> p t h c"),
                        PS[:, 2 * k:2 * k + 2, :].rearrange("p a n -> p (a n)")[:, 0:(t1 - t0) * CH]
                        .rearrange("p (t h c) -> p t h c", h=H1, c=D1)).then_inc(s_va, 1)

                def take_max(h, n0, n1):
                    for n_ in range(n0, n1):
                        dve.wait_ge(s_mx, (b * H1 + h) * MAX_UNITS + n_ + 1)
                        nc.vector.reduce_max(mxp[:, n_:n_ + 1], PS[:, 5 + n_ % 3, 0:GTOK], axis=AX.X).then_inc(s_mu, 1)

                def shift_pieces(h):
                    m = [0]
                    hd = b * H1 + h

                    def step(ins):
                        m[0] += 1
                        ins.then_inc(s_ch, 1)
                        dve.wait_ge(s_ch, hd * 5 + m[0])

                    dve.wait_ge(s_mu, hd * MAX_UNITS + MAX_UNITS)
                    step(nc.vector.tensor_reduce(nm, mxp.rearrange("p (t q) -> p t q", q=GROUPS), op=ALU.max,
                                                 axis=AX.X, negate=True))
                    step(nc.vector.tensor_copy(nmp[:, 0, :], nm))
                    step(nc.vector.tensor_tensor(nr, nm, nmp[:, 0, :], ALU.subtract))
                    step(nc.vector.tensor_copy(nmp[:, 1, :], nr))
                    step(nc.vector.tensor_tensor(nr, nr, nmp[:, 1, :], ALU.subtract))
                    nc.vector.tensor_copy(nmp[:, 2, :], nr).then_inc(s_nm, 1)
                    dve.wait_ge(s_nt, hd + 1)
                    nc.vector.tensor_copy(nmt[:], PS[0:3 * TILES, 5, 0:64].bitcast(bf16)).then_inc(s_nc, 1)

                def copy_half(h, half):
                    hd = b * H1 + h
                    dve.wait_ge(s_gpv, hd * EXP_UNITS + (half + 1) * EXP_UNITS // 2)
                    for k in range(H1):
                        dve.wait_ge(s_st[k], b * 192 + 192)
                    if half == 1:
                        dve.wait_ge(s_od, hd * 256 + 128)
                    nc.vector.tensor_copy(o_st[:, half, :], PS[:, 4, 0:GTOK]).then_inc(s_o, 1)

                take_max(0, 0, MAX_UNITS)
                shift_pieces(0)
                for h in range(H1 - 1):
                    take_max(h + 1, 0, MAX_HALF)
                    copy_half(h, 0)
                    take_max(h + 1, MAX_HALF, MAX_UNITS)
                    shift_pieces(h + 1)
                    copy_half(h, 1)
                copy_half(H1 - 1, 0)
                copy_half(H1 - 1, 1)

                dve.wait_ge(s_dl, b * 16 + 16)
                nc.vector.reciprocal(rdcomp, dcomp).then_inc(s_dr, 1)
                dve.wait_ge(s_al, b * 16 + 16)
                dve.wait_ge(s_rl, b * 64 + 64)
                for c in range(4):
                    sl = slice(c * PAIR, (c + 1) * PAIR)
                    nc.vector.tensor_tensor(T4[0:CH, sl], T4[0:CH, sl], T3[0:CH, sl], ALU.mult).then_inc(s_ao, 1)
                for g in range(GROUPS):
                    sl = slice(g * GTOK, (g + 1) * GTOK)
                    dve.wait_ge(s_fp, b * 8 + g + 1)
                    nc.vector.tensor_tensor(T2[0:CH, sl].rearrange("c (i w j) -> c w i j", i=WIN, j=WIN),
                                            PS[0:CH, g, 0:GTOK].rearrange("c (w i j) -> c w i j", i=WIN, j=WIN),
                                            z_w[:, sl].rearrange("c (w i j) -> c w i j", i=WIN, j=WIN),
                                            ALU.add).then_inc(s_fin, 1)

        @block.tensor
        def _(pe):
            mm = nc.tensor.matmul
            pe.wait_ge(s_w, 16 * NLOAD)
            pe.wait_ge(s_i2, 2)
            hot = [T2[:, 0:WTOK * WTOK], SP_[:, :, :].rearrange("p a n -> p (a n)")[:, 0:WTOK * WTOK]]
            NB = WTOK * WTOK // 7
            for c in range(7):
                sl = slice(c * NB, (c + 1) * NB)
                mm(PS[0:H0, c, 0:NB], tab[:, 0, :], hot[0][:, sl], start=True, stop=False)
                mm(PS[0:H0, c, 0:NB], tab[0:TABLE - 128, 1, :], hot[1][0:TABLE - 128, sl], start=False, stop=True)\
                    .then_inc(s_i3, 1)
            mm(PS[0:CH, 7, 0:1], w_p0c[:], bv0, start=True, stop=True).then_inc(s_i3, 1)
            pe.wait_ge(s_setup, 2)
            pe.wait_ge(s_i4, 7)
            pe.wait_ge(s_i1, 9)

            with pe.Fori(0, IMAGES) as b:
                pe.wait_ge(s_fin, b * 8 + 1)
                for c in range(4):
                    pe.wait_ge(s_xw, b * 8 + 2 * c + 2)
                    for i in range(2):
                        g = 2 * c + i
                        last = mm(PS[:, g, 0:GTOK], w_qk0[:], x_w[:, g * GTOK:(g + 1) * GTOK], start=True, stop=True)
                    last.then_inc(s_qk, 1)
                for c in range(4):
                    pe.wait_ge(s_sq, b * 8 + 2 * c + 2)
                    for i in range(2):
                        g = 2 * c + i
                        last = mm(PS[:, g, 0:GTOK], hsum[:], T3[:, g * GTOK:(g + 1) * GTOK], start=True, stop=True)
                    last.then_inc(s_ssq, 1)

                def scores(g):
                    pe.wait_ge(s_km[g % 2], b * 512 + (g // 2 + 1) * 128)
                    if g == 0:
                        pe.wait_ge(s_max, b * 4 + 4)
                    else:
                        pe.wait_ge(s_add, b * 8 + g)
                    wait_apart(pe, s_qn, b * 4 + min((g + 1) // 2 + 1, 4))
                    for w in range(8):
                        q0 = g * GTOK + w * WTOK
                        last = mm(PS[64 * (w % 2):64 * (w % 2) + 64, w // 2, 0:GTOK], T4[0:CH, q0:q0 + 64],
                                  kmask[:, g % 2, :, w * WTOK:(w + 1) * WTOK], start=True, stop=True)
                    last.then_inc(s_S, 1)

                def values(g):
                    if g >= 1:
                        pe.wait_ge(s_vb, b * 8 + g)
                    pe.wait_ge(s_x2, b * 8 + g + 1)
                    for w in range(8):
                        last = mm(PS[0:2 * WTOK, 6, w * CH:(w + 1) * CH],
                                  x_tw[:, g % 2, w, :, :].rearrange("c a m -> c (a m)"), w_v0[:],
                                  start=True, stop=True)
                    last.then_inc(s_V, 1)

                def transpose(g):
                    pe.wait_ge(s_P, b * 8 + g + 1)
                    for half in range(2):
                        if 2 * g + half >= 1:
                            pe.wait_ge(s_PT, b * 16 + 2 * g + half)
                        for p in range(2):
                            for q in range(4):
                                c0 = (2 * half + p) * GTOK + q * 2 * WTOK
                                last = nc.tensor.transpose(PS[0:2 * WTOK, 4 + p, q * 128:(q + 1) * 128],
                                                           Sb[:, g % 2, c0:c0 + 2 * WTOK], idf[:])
                        last.then_inc(s_T, 1)

                def attend(g):
                    pe.wait_ge(s_PT, b * 16 + 2 * g + 2)
                    pe.wait_ge(s_vb, b * 8 + g + 1)
                    if g >= 1:
                        pe.wait_ge(s_h1, b * 8 + g)
                    for w in range(8):
                        for q in range(4):
                            c0 = q * 128 + 64 * (w % 2)
                            last = mm(PS[32 * q:32 * q + 32, 7, w * WTOK:(w + 1) * WTOK], VB[:, g % 2, w, q, :],
                                      PT[0:2 * WTOK, g % 2, w // 2, c0:c0 + WTOK], start=True, stop=True)
                    last.then_inc(s_PV, 1)
                    pe.wait_ge(s_at, b * 8 + g + 1)
                    mm(PS[0:CH, 7, 0:GTOK], w_p0[:], T2[:, g * GTOK:(g + 1) * GTOK], start=True, stop=True)\
                        .then_inc(s_pr, 1)

                for g in range(GROUPS + 1):
                    if g < GROUPS:
                        scores(g)
                        values(g)
                    if g >= 1:
                        transpose(g - 1)
                        attend(g - 1)

                def group_mean_of(i):
                    wait_apart(pe, s_gq, b * 6 + 2 * i + 1)
                    mm(PS[0:CH, 6, 0:1], gmean[:], mv[:, 0:1], start=True, stop=True).then_inc(s_gr, 1)
                    wait_apart(pe, s_gq, b * 6 + 2 * i + 2)
                    mm(PS[0:CH, 6, 0:1], gmean[:], ge[:, 0:1], start=True, stop=True).then_inc(s_gr, 1)

                group_mean_of(0)
                group_mean_of(1)
                for c in range(9):
                    if c < 8:
                        pe.wait_ge(s_mi, b * 2 + c // 4 + 1)
                        if c >= 2:
                            pe.wait_ge(s_hid, b * 16 + 2 * c - 2)
                        for e in range(2):
                            last = mm(PS[:, 2 * (c % 2) + e, 0:GTOK], w_1[:, 128 * e:128 * e + 128],
                                      T2[0:CH, c * GTOK:(c + 1) * GTOK], start=True, stop=True)
                        last.then_inc(s_m1, 1)
                    if c >= 1:
                        k = c - 1
                        pe.wait_ge(s_hid, b * 16 + 2 * c)
                        if k >= 2:
                            pe.wait_ge(s_h2, b * 8 + k - 1)
                        for e in range(2):
                            last = mm(PS[0:CH, 4 + k % 2, 0:GTOK], w_2[:, e, :], hid[:, 2 * (k % 2) + e, 0:GTOK],
                                      start=(e == 0), stop=(e == 1))
                        last.then_inc(s_m2, 1)
                group_mean_of(2)

                pe.wait_ge(s_z, b * 2 + 2)
                for c in range(4):
                    for i in range(2):
                        g = 2 * c + i
                        last = mm(PS[:, g, 0:GTOK], w_qk1[:], z_w[:, g * GTOK:(g + 1) * GTOK], start=True, stop=True)
                    last.then_inc(s_gqk, 1)
                for t in range(TILES):
                    if t % 16 == 0:
                        pe.wait_ge(s_r, b * 4 + t // 16 + 1)
                    last = mm(PS[:, t // 8, (t % 8) * CH:(t % 8 + 1) * CH], z_w[:, t * 128:(t + 1) * 128], w_v1[:],
                              start=True, stop=True)
                    if t in (15, TILES - 1):
                        last.then_inc(s_gv, 1)

                def max_scores(h, n0, n1):
                    hd = b * H1 + h
                    for n_ in range(n0, n1):
                        if n_ >= 3:
                            pe.wait_ge(s_mu, hd * MAX_UNITS + n_ - 2)
                        mm(PS[:, 5 + n_ % 3, 0:GTOK], QS[0:STACK, h, (n_ // 8) * 128:(n_ // 8 + 1) * 128],
                           KS[0:STACK, h, (n_ % 8) * GTOK:(n_ % 8 + 1) * GTOK],
                           start=True, stop=True).then_inc(s_mx, 1)

                def shift_transposed(h):
                    pe.wait_ge(s_nm, b * H1 + h + 1)
                    nc.tensor.transpose(PS[0:3 * TILES, 5, 0:64].bitcast(bf16),
                                        nmp[:, :, :].rearrange("p c t -> p (c t)"), idb[:]).then_inc(s_nt, 1)

                def attend_head(h, with_next):
                    hd = b * H1 + h
                    pe.wait_ge(s_sh, hd * 48 + 48)
                    pe.wait_ge(s_ones, b * 2 + 2)
                    done = 0
                    for u in range(EXP_UNITS + 1):
                        if u < EXP_UNITS:
                            if u >= 2:
                                pe.wait_ge(s_ex, hd * EXP_UNITS + u - 1)
                            half, kt, i = u // (2 * TILES), (u // 2) % TILES, u % 2
                            for j in range(2):
                                c = 4 * half + 2 * i + j
                                last = mm(PS[:, 2 * (u % 2) + j, 0:GTOK],
                                          KS[0:STACK + SHIFT, h, kt * 128:(kt + 1) * 128],
                                          QS[0:STACK + SHIFT, h, c * GTOK:(c + 1) * GTOK], start=True, stop=True)
                            last.then_inc(s_gs, 1)
                        if with_next:
                            until = min(MAX_UNITS, (u + 1) * 20 // 9)
                            max_scores(h + 1, done, until)
                            if done < MAX_UNITS and until == MAX_UNITS:
                                shift_at = u + 3
                            done = until
                            if done == MAX_UNITS and u == shift_at:
                                shift_transposed(h + 1)
                        if u >= 1:
                            k = u - 1
                            half, kt, i = k // (2 * TILES), (k // 2) % TILES, k % 2
                            pe.wait_ge(s_ex, hd * EXP_UNITS + k + 1)
                            if k == EXP_UNITS // 2:
                                pe.wait_ge(s_o, hd * 2 + 1)
                            elif k == 0 and h > 0:
                                pe.wait_ge(s_o, hd * 2)
                            for j in range(2):
                                q0 = 32 * (2 * i + j)
                                last = mm(PS[q0:q0 + 32, 4, 0:GTOK], v_all[:, h, kt, :],
                                          E[:, k % 4, j * GTOK:(j + 1) * GTOK], start=(kt == 0), stop=(kt == TILES - 1))
                            last.then_inc(s_gpv, 1)

                pe.wait_ge(s_r, b * 4 + 4)
                pe.wait_ge(s_va, b * 2 + 2)
                for k in range(1):
                    pe.wait_ge(s_st[0], b * 192 + 192)
                max_scores(0, 0, MAX_UNITS)
                shift_transposed(0)
                for k in range(1, H1):
                    pe.wait_ge(s_st[k], b * 192 + 192)
                for h in range(H1 - 1):
                    attend_head(h, True)
                attend_head(H1 - 1, False)

                for g in range(GROUPS):
                    wait_apart(pe, s_ao, b * 4 + g // 2 + 1)
                    mm(PS[0:CH, g, 0:GTOK], w_p1[:], T4[0:CH, g * GTOK:(g + 1) * GTOK], start=True, stop=True)\
                        .then_inc(s_fp, 1)


def constants():
    import numpy as np

    head = np.arange(128) // D0
    group = np.arange(CH) // 4
    mask = np.repeat(np.arange(2), WTOK)[:, None] == np.repeat(np.arange(2), D0)[None, :]
    return {
        "ident": np.eye(128, dtype=np.float32),
        "head_sum": (head[:, None] == head[None, :]).astype(np.float32),
        "group_mean": (group[:, None] == group[None, :]).astype(np.float32) / 4,
        "head_mask": mask.astype(np.float32),
        "rows": np.stack([np.arange(128), np.arange(128) + 128], 1).astype(np.float32),
    }


_ORDER = ["x", "qkv_w", "qkv_b", "logit_scale", "bias_table", "rel_index", "proj_w", "proj_b", "gn1_w", "gn1_b",
          "gn2_w", "gn2_b", "mlp_gn_w", "mlp_gn_b", "mlp_w1", "mlp_b1", "mlp_w2", "mlp_b2"]
_TRANSPOSED = {"qkv_w", "proj_w", "mlp_w1", "mlp_w2"}


def kernel(**inputs):
    import numpy as np
    import concourse.bacc as bacc
    from concourse.bass_utils import run_bass_kernel_spmd as run

    given = {"x": np.asarray(inputs["x"]).reshape(IMAGES, CH, TOKENS)}
    for name in _ORDER[1:]:
        a = np.asarray(inputs["L0_conv_" + name])
        given[name] = a.T if name in _TRANSPOSED else a
    for name in ("w_qkv", "w_proj"):
        given[name] = np.asarray(inputs["L1_conv_" + name]).T
    given.update(constants())

    nc = bacc.Bacc("TRN2", target_bir_lowering=False, num_devices=1)
    arrays, args = {}, []
    for name, a in given.items():
        a = np.ascontiguousarray(a)
        arrays["in_" + name] = a
        args.append(nc.dram_tensor("in_" + name, a.shape, mybir.dt.from_np(a.dtype), kind="ExternalInput").ap())
    f32 = mybir.dt.float32
    args.append(nc.dram_tensor("out_0", [IMAGES, CH, TOKENS], f32, kind="ExternalOutput").ap())
    for name, shape in (("scratch_bias", [H0, WTOK * WTOK]), ("scratch_att", [CH, TOKENS]),
                        ("scratch_den", [H1, TOKENS]), ("scratch_rden", [H1, TOKENS])):
        args.append(nc.dram_tensor(name, shape, f32, kind="Internal").ap())
    nc.disable_value_cache = True
    attention_mlp_kernel(nc, *args)
    r = run(nc, [arrays], core_ids=[0])
    return r.results[0]["out_0"].reshape(IMAGES, CH, RES, RES)
```

```python
import concourse.bass as bass
from concourse import mybir
from contextlib import ExitStack

IMAGES, CH, RES, WIN = 16, 64, 56, 7
TOKENS = RES * RES
WTOK = WIN * WIN
GROUPS = RES // WIN
GTOK = TOKENS // GROUPS
H0, D0 = 8, 8
H1, D1 = 4, 16
HID = 256
TABLE = (2 * WIN - 1) ** 2
TILES = -(-TOKENS // 128)
PADTOK = TILES * 128
PAIR = 2 * GTOK
PIECES = 6
STACK = PIECES * D1
SHIFT = 3
HALF = TOKENS // 2
STAGES = 2 * H1
EXP_UNITS = TILES * 2
PV_LAG = 2
STAGE_TILES = ((0, -(-TILES // 2)), (-(-TILES // 2), TILES))
FIRST_QUADS = 2 * STAGE_TILES[0][1]
MAX_LEAD, MAX_RATE = 14, 2.04
FIRST_LAG, SHIFT_LAG = 3, 6
EARLY = 2
ROOT_UNIT = 23


def maxima_schedule():
    slots = []
    for stage in range(1, STAGES):
        count = 0
        for tile in range(*STAGE_TILES[stage % 2]):
            for chunk in range(GROUPS):
                slots.append((stage, tile, chunk))
                count += 1
                if count == (FIRST_LAG if stage == 1 else SHIFT_LAG):
                    slots.append((stage - 1, None, None))
    slots.append((STAGES - 1, None, None))
    return slots


MAXIMA = maxima_schedule()
RING = len(MAXIMA)
SIDE_BANKS = [5 + k % 3 for k in range(22)]


def maxima_before(unit):
    return min(RING, MAX_LEAD + int(MAX_RATE * unit))


LN100 = 4.605170185988092


def attention_mlp_kernel(nc, x, qkv0, qkv0_b, logit_scale, table, rel_index, proj0, proj0_b, gn1_w, gn1_b,
                         gn2_w, gn2_b, gnm_w, gnm_b, w1, b1, w2, b2, qkv1, proj1,
                         ident, head_sum, head_spread, group_mean, head_mask, query_ident, rows,
                         out, scratch_bias, scratch_att,
                         scratch_rden):
    f32, bf16, i32 = mybir.dt.float32, mybir.dt.bfloat16, mybir.dt.int32
    ALU, ACT, AX = mybir.AluOpType, mybir.ActivationFunctionType, mybir.AxisListType

    ctx = ExitStack()
    with ctx:
        def sb(name, shape, dt=f32):
            return ctx.enter_context(nc.sbuf_tensor(name, shape, dt))

        def sem(name):
            return ctx.enter_context(nc.semaphore(name))

        w_qk0 = sb("w_qk0", [CH, 128])
        w_v0 = sb("w_v0", [CH, CH])
        w_p0 = sb("w_p0", [128, CH])
        w_p0c = sb("w_p0c", [CH, CH])
        w_1 = sb("w_1", [CH, HID])
        w_2 = sb("w_2", [128, 2, CH])
        w_qk1 = sb("w_qk1", [CH, 128])
        w_v1 = sb("w_v1", [CH, CH])
        w_p1 = sb("w_p1", [CH, CH])
        vec = sb("vec", [128, 24])
        bqk0, pb0, bv0, b2c = vec[:, 0:1], vec[0:CH, 1:2], vec[0:CH, 2:3], vec[0:CH, 3:4]
        b1c = [vec[:, 4:5], vec[:, 5:6]]
        gn_w = [vec[0:CH, 6 + 2 * i:7 + 2 * i] for i in range(3)]
        gn_b = [vec[0:CH, 7 + 2 * i:8 + 2 * i] for i in range(3)]
        qkscale, rows_c = vec[:, 12:13], vec[:, 13:15]
        scale_raw, minus_half = vec[:, 15:16], vec[:, 16:17]
        pbias = vec[0:CH, 17:18]
        ident_f32 = sb("ident_f32", [128, 128])
        ident_bf16 = sb("ident_bf16", [128, 128], bf16)
        w_head_sum = sb("w_head_sum", [128, 32])
        w_spread = sb("w_spread", [128, 4, 128])
        w_group_mean = sb("gmean", [CH, CH])
        v_head_mask = sb("vmask", [2 * WTOK, 2 * D0])
        bias_table = sb("tab", [128, 2, H0])

        x_in = sb("x_in", [CH, TOKENS])
        x_w = sb("x_w", [CH, PADTOK])
        tok_qk = sb("tok_qk", [128, TOKENS])
        tok_h = sb("tok_h", [128, TOKENS])
        tok_unit = sb("tok_unit", [128, PADTOK])
        z_w = sb("z_w", [CH, PADTOK])
        kmask = sb("kmask", [128, 2, H0, GTOK])
        scores_buf = sb("scores_buf", [128, 4, PAIR])
        values_buf = sb("values_buf", [128, 2, 4, 512])
        win_v = sb("win_v", [2 * WTOK, 2, 8, 4, 32])
        piece_l = sb("piece_l", [128, TOKENS], bf16)
        pieces = [tok_qk[:, :].bitcast(bf16)[:, 0:TOKENS], tok_qk[:, :].bitcast(bf16)[:, TOKENS:2 * TOKENS],
                    piece_l[:, :]]
        q_stack = sb("q_stack", [128, H1, PADTOK], bf16)
        k_stack = sb("k_stack", [128, H1, PADTOK], bf16)
        small = sb("small", [128, 256])
        neg_rows = sb("neg_rows", [3 * TILES, 128], bf16)
        neg_pieces = sb("neg_pieces", [128, 3 * TILES], bf16)

        win_scores = scores_buf[:, :, :].rearrange("p (b c) n -> p b (c n)", b=2)
        hidden = scores_buf[:, :, :]
        exps = scores_buf[:, :, :]
        win_probs_t = values_buf
        v_all = values_buf[:, :, :, :].rearrange("p a b n -> p (a b n)")[:, 0:H1 * TILES * 32]
        v_all = v_all.rearrange("p (h t c) -> p h t c", h=H1, t=TILES)
        x_tw = sb("x_tw", [CH, 2, 8, 2, WTOK])
        sp_flat = scores_buf[:, :, :].rearrange("p a n -> p (a n)")
        pv_flat = values_buf[:, :, :, :].rearrange("p a b n -> p (a b n)")
        v_cols = H1 * TILES * 32
        o_st = pv_flat[:, v_cols:v_cols + 2 * GTOK].rearrange("p (a n) -> p a n", a=2)
        free_head = [q_stack[0:CH, h, 0:TOKENS].bitcast(f32) for h in range(3)]
        att = [tok_unit[0:CH, 0:HALF], free_head[0]]
        inv_sums = [x_tw[:, :, :, :, :].rearrange("c s w a m -> c (s w a m)"), free_head[1]]
        result = [piece_l[0:CH, :].bitcast(f32), free_head[2]]
        win_neg_max, den, rden = small[:, 0:32], small[:, 32:64], small[:, 64:96]
        stats = small[0:CH, 96:144].rearrange("p (c s) -> p c s", c=8)
        mv, gd, ge, gt, gp, gA, gB = (small[0:CH, 144 + 4 * i:146 + 4 * i] for i in range(7))
        max_parts = small[:, 0:TILES * GROUPS]
        neg_max = small[:, 200:225]
        neg_rest = small[:, 225:250]
        sums_compact = small[:, 96:145]
        inv_compact = small[:, 145:194]

        PS = ctx.enter_context(nc.psum_tensor("PS", [128, 8, 512], f32))

        s_weights, s_scale_loaded = sem("weights_loaded"), sem("scale_loaded")
        s_w_zeroed, s_zeroed, s_onehot, s_bias_product, s_bias_copied, s_scale_bounded, s_scale_exp = (
            sem(n) for n in ("w_zeroed", "zeroed", "onehot", "bias_product", "bias_copied", "scale_bounded",
                             "scale_exp"))
        s_bias_stored, s_bias_loaded = sem("bias_stored"), sem("bias_loaded")
        s_setup = sem("setup_chain")
        s_x_loaded, s_x_by_windows, s_x_twice = sem("x_loaded"), sem("x_by_windows"), sem("x_twice")
        (s_qk_product, s_qk_biased, s_qk_squares, s_head_sums, s_sums_bounded, s_norms, s_norms_inverted,
         s_norms_spread, s_qk_normalised) = (sem(n) for n in (
            "qk_product", "qk_biased", "qk_squares", "head_sums", "sums_bounded", "norms", "norms_inverted",
            "norms_spread", "qk_normalised"))
        s_kmask = [sem("kmask_even"), sem("kmask_odd")]
        s_queries = [sem("queries_even"), sem("queries_odd")]
        s_win_scores, s_win_shifted, s_win_exps, s_win_probs, s_win_v, s_win_v_blocks = (sem(n) for n in (
            "win_scores", "win_shifted", "win_exps", "win_probs", "win_v", "win_v_blocks"))
        s_win_transposed, s_win_transposed_copied, s_win_pv, s_win_att, s_win_proj, s_residual1 = (sem(n) for n in (
            "win_transposed", "win_transposed_copied", "win_pv", "win_att", "win_proj", "residual1"))
        s_gn_request, s_gn_mean, s_pow_request, s_pow_done, s_gn_affine = (sem(n) for n in (
            "gn_request", "gn_mean", "pow_request", "pow_done", "gn_affine"))
        s_h_ready, s_mlp_in, s_mlp1, s_hidden, s_mlp2, s_residual2, s_z_ready = (sem(n) for n in (
            "h_ready", "mlp_in", "mlp1", "hidden", "mlp2", "residual2", "z_ready"))
        s_gqk, s_piece_h, s_rest, s_piece_m, s_piece_l, s_gv, s_v_all_ready, s_ones_set = (sem(n) for n in (
            "gqk", "piece_h", "rest", "piece_m", "piece_l", "gv", "v_all_ready", "ones_set"))
        s_stacks = [sem(f"stacks_loaded{h}") for h in range(H1)]
        s_quad_filled, s_quad_emptied, s_slot_filled, s_slot_emptied, s_max_pieces, s_shift_loaded = (sem(n) for n in (
            "max_quad_filled", "max_quad_emptied", "max_slot_filled", "max_slot_emptied", "max_pieces", "shift_loaded"))
        s_scores, s_exps, s_pv_done, s_out_copied, s_out_stored = (sem(n) for n in (
            "scores", "exps", "pv_done", "out_copied", "out_stored"))
        (s_att_loaded, s_den_loaded, s_den_inverted, s_rden_stored, s_rden_loaded, s_att_scaled, s_final_proj,
         s_final, s_out_written) = (sem(n) for n in (
            "att_loaded", "den_loaded", "den_inverted", "rden_stored", "rden_loaded", "att_scaled",
            "final_proj", "final", "out_written"))
        s_out_written = [s_out_written, sem("out_written2")]
        s_dve_chain, s_shift_chain = sem("dve_chain"), sem("dve_shift_chain")
        CHAIN = 60

        def att_bank(g):
            return SIDE_BANKS[10 + g] if g < 4 else 4 + g % 2

        def wait_apart(eng, semaphore, value):
            if not isinstance(value, int):
                value = eng.to_reg(value)
                eng.wait_ge(s_zeroed, 9)
            eng.wait_ge(semaphore, value)

        block = ctx.enter_context(nc.Block())
        NLOAD = 33

        @block.sync
        def _(sp):
            def load(dst, src, s=s_weights):
                sp.dma_start(dst, src).then_inc(s, 16)

            col = lambda v: v.rearrange("(n o) -> n o", o=1)
            load(tok_h[:, 0:WTOK * WTOK].bitcast(i32), rel_index.rearrange("n m -> (n m)").partition_broadcast(128))
            load(bias_table[:, 0, :], table[0:128, :])
            load(bias_table[0:TABLE - 128, 1, :], table[128:TABLE, :])
            load(rows_c, rows)
            load(w_qk0[:], qkv0[:, 0:128])
            load(w_v0[:], qkv0[:, 128:192])
            sp.wait_ge(s_w_zeroed, 1)
            for p in range(4):
                load(w_p0[32 * p:32 * p + 16, :], proj0[16 * p:16 * p + 16, :])
            load(w_p0c[:], proj0)
            load(w_1[:], w1)
            load(w_2[:], w2.rearrange("(a p) c -> p a c", a=2))
            load(w_qk1[:], qkv1[:, 0:128])
            load(w_v1[:], qkv1[:, 128:192])
            load(w_p1[:], proj1)
            load(bqk0, col(qkv0_b[0:128]))
            load(bv0, col(qkv0_b[128:192]))
            load(pb0, col(proj0_b))
            load(b2c, col(b2))
            load(b1c[0], col(b1[0:128]))
            load(b1c[1], col(b1[128:256]))
            for i, (w_, b_) in enumerate(((gn1_w, gn1_b), (gnm_w, gnm_b), (gn2_w, gn2_b))):
                load(gn_w[i], col(w_))
                load(gn_b[i], col(b_))
            load(ident_f32[:], ident)
            load(w_head_sum[:], head_sum)
            load(w_spread[:], head_spread)
            load(w_group_mean[:], group_mean)
            load(v_head_mask[:], head_mask)
            for h in range(H0):
                load(scale_raw[CH + D0 * h:CH + D0 * h + D0, :],
                     logit_scale[h:h + 1].partition_broadcast(D0), s_scale_loaded)
            sp.wait_ge(s_bias_copied, 7)
            sp.dma_start(scratch_bias, tok_unit[0:H0, 0:WTOK * WTOK]).then_inc(s_bias_stored, 16)
            sp.wait_ge(s_bias_stored, 16)
            sp.wait_ge(s_zeroed, 9)
            for slot in range(2):
                for w in range(8):
                    sp.dma_start(kmask[CH:CH + WTOK, slot, :, w * WTOK:(w + 1) * WTOK],
                                 scratch_bias.rearrange("h (n m) -> n h m", n=WTOK))\
                      .then_inc(s_out_written[slot] if w == 7 else s_bias_loaded, 16)
            sp.dma_start(x_in[:], x[0, :, :]).then_inc(s_x_loaded, 16)

            def load_k(t, g):
                sp.wait_ge(s_qk_normalised, t * 8 + g + 1)
                for h in range(H0):
                    sp.dma_start(kmask[D0 * h:D0 * h + D0, g % 2, h, :],
                                 tok_unit[CH + D0 * h:CH + D0 * h + D0, g * GTOK:(g + 1) * GTOK])\
                      .then_inc(s_kmask[g % 2], 16)

            def set_queries(t, g):
                sp.wait_ge(s_kmask[g % 2], t * 512 + (g // 2 + 1) * 128)
                sp.dma_start(tok_unit[CH:CH + WTOK, g * GTOK:(g + 1) * GTOK], query_ident)\
                  .then_inc(s_queries[g % 2], 16)

            def next_k(t, g):
                sp.wait_ge(s_win_scores, t * 8 + g - 1)
                load_k(t, g)
                set_queries(t, g)

            for g in range(2):
                load_k(0, g)
                set_queries(0, g)
            next_k(0, 2)
            with sp.Fori(0, IMAGES) as b:
                sp.wait_ge(s_x_by_windows, b * 8 + 8)
                sp.dma_start(x_in[:], x[bass.ds((b + 1) % IMAGES, 1), :, :].rearrange("o c n -> (o c) n"))\
                  .then_inc(s_x_loaded, 16)
                for g in range(3, GROUPS):
                    next_k(b, g)
                sp.wait_ge(s_piece_l, b * 4 + 4)
                sp.wait_ge(s_piece_m, b * 4 + 4)
                sp.wait_ge(s_out_written[1], b * 16 + 16)
                for h in range(H1):
                    for dst, base, order in ((q_stack, 0, (0, 0, 1, 1, 0, 2)), (k_stack, CH, (0, 1, 0, 1, 2, 0))):
                        for j, pc in enumerate(order):
                            sp.dma_start(dst[D1 * j:D1 * j + D1, h, 0:TOKENS],
                                         pieces[pc][base + D1 * h:base + D1 * h + D1, :]).then_inc(s_stacks[h], 16)

                def shift_rows(stage):
                    t0, t1 = STAGE_TILES[stage % 2]
                    sp.wait_ge(s_slot_emptied, b * RING + MAXIMA.index((stage, None, None)) + 1)
                    for pc in range(3):
                        sp.dma_start(q_stack[STACK + pc:STACK + pc + 1, stage // 2, t0 * 128:t1 * 128]
                                     .rearrange("p (t n) -> p t n", n=128),
                                     neg_rows[(t1 - t0) * pc:(t1 - t0) * (pc + 1), :]).then_inc(s_shift_loaded, 16)

                def store_half(stage):
                    h, half = stage // 2, stage % 2
                    sp.wait_ge(s_out_copied, b * STAGES + stage + 1)
                    for j in range(4):
                        sl = slice(j * GTOK, (j + 1) * GTOK)
                        sp.dma_start(scratch_att[half, h, :, sl], o_st[32 * j:32 * j + D1 + 1, half, :])\
                          .then_inc(s_out_stored, 16)
                    wait_apart(sp, s_out_stored, (b * STAGES + stage + 1) * 64)

                def invert_sums(half):
                    sp.dma_start(sums_compact, scratch_att[half, :, D1, :].rearrange("h (a n) -> h a n", a=32))\
                      .then_inc(s_den_loaded, 16)
                    sp.dma_start(att[half], scratch_att[half, :, 0:D1, :]).then_inc(s_att_loaded, 16)
                    sp.wait_ge(s_den_inverted, b * 2 + half + 1)
                    sp.dma_start(scratch_rden[half, :, :].rearrange("h (a n) -> (h a) n", a=32), inv_compact)\
                      .then_inc(s_rden_stored, 16)
                    sp.wait_ge(s_rden_stored, b * 32 + half * 16 + 16)
                    for h in range(H1):
                        sp.dma_start(inv_sums[half][D1 * h:D1 * h + D1, :],
                                     scratch_rden[half, h, :].partition_broadcast(D1)).then_inc(s_rden_loaded, 16)

                def write_out(half):
                    sp.wait_ge(s_final, b * 8 + 4 * half + 5)
                    sp.dma_start(out[bass.ds(b, 1), :, half * HALF:(half + 1) * HALF]
                                 .rearrange("o c n -> (o c) n"), result[half]).then_inc(s_out_written[half], 16)

                shift_rows(0)
                for stage in range(STAGES):
                    if stage + 1 < STAGES:
                        shift_rows(stage + 1)
                    store_half(stage)
                    if stage == STAGES - 2:
                        invert_sums(0)
                        write_out(0)
                        for g in range(2):
                            load_k(b + 1, g)
                            set_queries(b + 1, g)
                invert_sums(1)
                next_k(b + 1, 2)
                write_out(1)
            sp.wait_ge(s_out_written[0], 16 * IMAGES + 16)
            sp.wait_ge(s_out_written[1], 16 * IMAGES + 16)
            for i in range(2):
                sp.wait_ge(s_queries[i], 64 * IMAGES + (32, 16)[i])

        @block.gpsimd
        def _(pl):
            nc.gpsimd.memset(w_p0[:], 0.0).then_inc(s_w_zeroed, 1)
            nc.gpsimd.memset(x_w[:], 0.0).then_inc(s_zeroed, 1)
            nc.gpsimd.memset(kmask[:], 0.0).then_inc(s_zeroed, 1)
            nc.gpsimd.memset(win_v[:], 0.0).then_inc(s_zeroed, 1)
            nc.gpsimd.memset(z_w[:, TOKENS:PADTOK], 0.0).then_inc(s_zeroed, 1)
            nc.gpsimd.memset(tok_unit[:, TOKENS:PADTOK], 0.0).then_inc(s_zeroed, 1)
            nc.gpsimd.memset(q_stack[:], 0.0).then_inc(s_zeroed, 1)
            nc.gpsimd.memset(k_stack[:], 0.0).then_inc(s_zeroed, 1)
            pl.wait_ge(s_zeroed, 7)
            nc.gpsimd.memset(k_stack[STACK:STACK + SHIFT, :, 0:TOKENS], 1.0).then_inc(s_zeroed, 1)
            pl.wait_ge(s_zeroed, 8)
            nc.gpsimd.memset(minus_half, -0.5).then_inc(s_zeroed, 1)

            def reorder(n):
                for g in range(GROUPS):
                    src = x_in[:, g * GTOK:(g + 1) * GTOK].rearrange("c (i w j) -> c w i j", i=WIN, j=WIN)
                    dst = x_w[:, g * GTOK:(g + 1) * GTOK].rearrange("c (w i j) -> c w i j", i=WIN, j=WIN)
                    nc.gpsimd.tensor_copy(dst, src).then_inc(s_x_by_windows, 1)

            pl.wait_ge(s_x_loaded, 16)
            reorder(0)

            def twice(g):
                src = x_w[:, g * GTOK:(g + 1) * GTOK].rearrange("c (w m) -> c w m", m=WTOK)
                nc.gpsimd.tensor_copy(x_tw[:, g % 2, :, :, :], src.unsqueeze(2).broadcast_to([CH, 8, 2, WTOK]))\
                  .then_inc(s_x_twice, 1)

            def first_twice(t):
                wait_apart(pl, s_qk_normalised, t * 8 + 8)
                wait_apart(pl, s_x_by_windows, t * 8 + 8)
                for g in range(2):
                    twice(g)

            first_twice(0)
            with pl.Fori(0, IMAGES) as b:
                for g in range(2, GROUPS):
                    wait_apart(pl, s_win_v, b * 8 + g - 1)
                    twice(g)
                for i in range(3):
                    pl.wait_ge(s_pow_request, b * 3 + i + 1)
                    nc.gpsimd.tensor_tensor(gp[:, 0:1], gt[:, 0:1], minus_half[0:CH, :], ALU.pow)\
                      .then_inc(s_pow_done, 1)
                wait_apart(pl, s_win_pv, b * 8 + 8)
                nc.gpsimd.memset(v_all[:, :, :, D1:32], 1.0).then_inc(s_ones_set, 1)
                wait_apart(pl, s_ones_set, b * 2 + 1)
                nc.gpsimd.memset(v_all[TOKENS % 128:128, :, TILES - 1, D1:32], 0.0).then_inc(s_ones_set, 1)
                pl.wait_ge(s_x_loaded, b * 16 + 32)
                wait_apart(pl, s_residual1, b * 8 + 8)
                reorder(b + 1)
                first_twice(b + 1)

        @block.scalar
        def _(act):
            def pair(t, c):
                return t[:, c * PAIR:(c + 1) * PAIR].rearrange("p (a n) -> p a n", a=2)

            act.wait_ge(s_scale_bounded, 1)
            nc.scalar.activation(qkscale[CH:128, :], scale_raw[CH:128, :], ACT.Exp).then_inc(s_scale_exp, 1)
            act.wait_ge(s_weights, 16 * NLOAD)

            def norms(t):
                act.wait_ge(s_sums_bounded, t * 2 + 2)
                nc.scalar.activation(tok_h[:, 0:2 * GTOK], tok_h[:, 0:2 * GTOK], ACT.Sqrt).then_inc(s_norms, 1)

            def window_exps(t, g):
                act.wait_ge(s_win_shifted, t * 8 + g + 1)
                nc.scalar.activation(win_scores[:, g % 2, :], win_scores[:, g % 2, :], ACT.Exp).then_inc(s_win_exps, 1)

            def copy_transposed(t, g):
                for half in range(2):
                    act.wait_ge(s_win_transposed, t * 16 + 2 * g + half + 1)
                    if g >= 2:
                        act.wait_ge(s_win_pv, t * 8 + g - 1)
                    nc.scalar.activation(win_probs_t[0:2 * WTOK, g % 2, 2 * half:2 * half + 2, :],
                                         PS[0:2 * WTOK, 4:6, :], ACT.Copy).then_inc(s_win_transposed_copied, 1)

            def copy_attention(t, g):
                act.wait_ge(s_win_pv, t * 8 + g + 1)
                nc.scalar.activation(tok_qk[:, g * GTOK:(g + 1) * GTOK], PS[:, 7, 0:GTOK], ACT.Copy)\
                  .then_inc(s_win_att, 1)

            def first_groups(t):
                window_exps(t, 0)
                copy_transposed(t, 0)
                window_exps(t, 1)
                copy_attention(t, 0)

            norms(0)
            first_groups(0)
            with act.Fori(0, IMAGES) as b:
                for g in range(2, GROUPS + 1):
                    copy_transposed(b, g - 1)
                    if g < GROUPS:
                        window_exps(b, g)
                    copy_attention(b, g - 1)
                for src, dst, fn, s, i in ((tok_h, tok_h, ACT.Relu, s_h_ready, 0),
                            (tok_h, tok_qk, ACT.Identity, s_mlp_in, 1)):
                    act.wait_ge(s_gn_affine, b * 3 + i + 1)
                    for a in range(2):
                        nc.scalar.activation(dst[0:CH, a * HALF:(a + 1) * HALF], src[0:CH, a * HALF:(a + 1) * HALF],
                                             fn, bias=gB[:, 0:1], scale=gA[:, 0:1]).then_inc(s, 1)
                for c in range(GROUPS):
                    act.wait_ge(s_mlp1, b * 8 + c + 1)
                    if c >= 2:
                        act.wait_ge(s_mlp2, b * 8 + c - 1)
                    for e in range(2):
                        nc.scalar.activation(hidden[:, 2 * (c % 2) + e, 0:GTOK], PS[:, 2 * (c % 2) + e, 0:GTOK],
                                             ACT.Relu, bias=b1c[e]).then_inc(s_hidden, 1)
                act.wait_ge(s_gn_affine, b * 3 + 3)
                for a in range(2):
                    nc.scalar.activation(z_w[:, a * HALF:(a + 1) * HALF], tok_h[0:CH, a * HALF:(a + 1) * HALF],
                                         ACT.Relu, bias=gB[:, 0:1], scale=gA[:, 0:1]).then_inc(s_z_ready, 1)
                for c in range(5):
                    if c < 4:
                        act.wait_ge(s_gqk, b * 4 + c + 1)
                        nc.scalar.activation(pair(pieces[0], c), PS[:, 2 * c:2 * c + 2, 0:GTOK], ACT.Copy)\
                          .then_inc(s_piece_h, 1)
                    if c >= 1:
                        act.wait_ge(s_rest, b * 4 + c)
                        nc.scalar.activation(pair(pieces[1], c - 1), pair(tok_h, c - 1), ACT.Copy)\
                          .then_inc(s_piece_m, 1)
                for u in range(STAGES * EXP_UNITS):
                    act.wait_ge(s_scores, b * STAGES * EXP_UNITS + u + 1)
                    if u >= 4:
                        act.wait_ge(s_pv_done, b * STAGES * EXP_UNITS + u - 3)
                    nc.scalar.activation(exps[:, u % 4, :].rearrange("p (a n) -> p a n", a=2),
                                         PS[:, 2 * (u % 2):2 * (u % 2) + 2, 0:GTOK], ACT.Exp,
                                         scale=D1 ** -0.5).then_inc(s_exps, 1)
                    if u == (STAGES - 1) * EXP_UNITS + ROOT_UNIT:
                        norms(b + 1)
                first_groups(b + 1)

        @block.vector
        def _(dve):
            def pair(t, c):
                return t[:, c * PAIR:(c + 1) * PAIR].rearrange("p (a n) -> p a n", a=2)

            dve.wait_ge(s_weights, 16 * NLOAD)
            dve.wait_ge(s_scale_loaded, 16 * H0)
            nc.vector.tensor_scalar(scale_raw[CH:128, :], scale_raw[CH:128, :], LN100, None, ALU.min)\
              .then_inc(s_scale_bounded, 1)
            nc.vector.memset(qkscale[0:CH, :], 1.0).then_inc(s_setup, 1)
            nc.vector.tensor_copy(ident_bf16[:], ident_f32[:]).then_inc(s_setup, 1)
            rel = tok_h[:, 0:WTOK * WTOK].bitcast(i32)
            hot = [tok_qk[:, 0:WTOK * WTOK], scores_buf[:, :, :].rearrange("p a n -> p (a n)")[:, 0:WTOK * WTOK]]
            for r in range(2):
                nc.vector.tensor_scalar(hot[r], rel, rows_c[:, r:r + 1], None, ALU.is_equal).then_inc(s_onehot, 1)
            NB = WTOK * WTOK // 7
            for c in range(7):
                dve.wait_ge(s_bias_product, c + 1)
                nc.vector.tensor_copy(tok_unit[0:H0, c * NB:(c + 1) * NB], PS[0:H0, c, 0:NB]).then_inc(s_bias_copied, 1)
            dve.wait_ge(s_bias_product, 8)
            nc.vector.tensor_tensor(pbias, PS[0:CH, 7, 0:1], pb0, ALU.add).then_inc(s_final, 1)
            dve.wait_ge(s_setup, 2)
            dve.wait_ge(s_final, 1)
            dve.wait_ge(s_scale_exp, 1)
            dve.wait_ge(s_zeroed, 9)
            dve.wait_ge(s_bias_stored, 16)
            for half in range(2):
                dve.wait_ge(s_out_written[half], 16)
            nc.vector.memset(PS[96:128, 3, 0:GTOK], 0.0).then_inc(s_setup, 1)

            def square_qk(t, g):
                sl = slice(g * GTOK, (g + 1) * GTOK)
                dve.wait_ge(s_qk_product, t * 8 + g + 1)
                nc.vector.tensor_scalar(tok_qk[:, sl], PS[:, SIDE_BANKS[g], 0:GTOK], bqk0, None, ALU.add)\
                  .then_inc(s_qk_biased, 1)
                dve.wait_ge(s_qk_biased, t * 8 + g + 1)
                nc.vector.tensor_tensor(tok_h[:, sl], tok_qk[:, sl], tok_qk[:, sl], ALU.mult).then_inc(s_qk_squares, 1)

            def bound_sums(t):
                for r in range(2):
                    dve.wait_ge(s_head_sums, t * 2 + r + 1)
                    nc.vector.tensor_scalar(tok_h[:, r * GTOK:(r + 1) * GTOK], PS[:, SIDE_BANKS[8 + r], 0:GTOK],
                                            1e-24, None, ALU.max).then_inc(s_sums_bounded, 1)

            def invert_norms(t):
                dve.wait_ge(s_norms, t + 1)
                for r in range(2):
                    sl = slice(r * GTOK, (r + 1) * GTOK)
                    nc.vector.reciprocal(tok_h[:, sl], tok_h[:, sl]).then_inc(s_norms_inverted, 1)

            def normalise_qk(t):
                for g in range(GROUPS):
                    sl = slice(g * GTOK, (g + 1) * GTOK)
                    dve.wait_ge(s_norms_spread, t * 8 + g + 1)
                    nc.vector.scalar_tensor_tensor(out=tok_unit[:, sl], in0=tok_qk[:, sl], scalar=qkscale,
                                                   in1=PS[:, SIDE_BANKS[14 + g], 0:GTOK],
                                                   op0=ALU.mult, op1=ALU.mult).then_inc(s_qk_normalised, 1)

            def shift(t, g, link):
                scores = PS[:, 0:4, 0:GTOK].rearrange("p a (h m) -> p a h m", m=WTOK)
                nmx4 = win_neg_max.rearrange("p (a h) -> p a h", a=4)
                dve.wait_ge(s_win_scores, t * 8 + g + 1)
                link(nc.vector.tensor_reduce(nmx4, scores, op=ALU.max, axis=AX.X, negate=True))
                if g >= 2:
                    dve.wait_ge(s_win_transposed, t * 16 + 2 * (g - 1))
                nc.vector.tensor_tensor(win_scores[:, g % 2, :].rearrange("p (a h m) -> p a h m", a=4, m=WTOK), scores,
                                        nmx4.unsqueeze(3).broadcast_to([128, 4, H0, WTOK]), ALU.add)\
                  .then_inc(s_win_shifted, 1)

            def v_blocks(t, g):
                dve.wait_ge(s_win_v, t * 8 + g + 1)
                if g >= 2:
                    dve.wait_ge(s_win_pv, t * 8 + g - 1)
                nc.vector.tensor_tensor(win_v[:, g % 2, :, :, 0:2 * D0].rearrange("p w q c -> p (w q) c"),
                                        PS[0:2 * WTOK, 6, :].rearrange("p (a c) -> p a c", c=2 * D0),
                                        v_head_mask[:].unsqueeze(1).broadcast_to([2 * WTOK, 32, 2 * D0]), ALU.mult)\
                  .then_inc(s_win_v_blocks, 1)

            def normalise(t, g, link):
                S3 = win_scores[:, g % 2, :].rearrange("p (a m) -> p a m", m=WTOK)
                dve.wait_ge(s_win_exps, t * 8 + g + 1)
                link(nc.vector.reduce_sum(den, S3, axis=AX.X))
                link(nc.vector.reciprocal(rden, den))
                nc.vector.tensor_tensor(S3, S3, rden.unsqueeze(2).broadcast_to([128, 32, WTOK]), ALU.mult)\
                  .then_inc(s_win_probs, 1)

            first_n = [0]

            def first_link(ins):
                first_n[0] += 1
                ins.then_inc(s_dve_chain, 1)
                dve.wait_ge(s_dve_chain, first_n[0])

            for g in range(GROUPS):
                square_qk(0, g)
            bound_sums(0)
            invert_norms(0)
            normalise_qk(0)
            shift(0, 0, first_link)
            v_blocks(0, 0)
            normalise(0, 0, first_link)
            shift(0, 1, first_link)
            v_blocks(0, 1)
            with dve.Fori(0, IMAGES) as b:
                n = [first_n[0]]

                def link(ins):
                    n[0] += 1
                    ins.then_inc(s_dve_chain, 1)
                    dve.wait_ge(s_dve_chain, b * CHAIN + n[0])

                def residual(g):
                    sl = slice(g * GTOK, (g + 1) * GTOK)
                    dve.wait_ge(s_win_proj, b * 8 + g + 1)
                    nc.vector.scalar_tensor_tensor(out=tok_h[0:CH, sl], in0=PS[0:CH, 7, 0:GTOK], scalar=pbias,
                                                   in1=x_w[:, sl], op0=ALU.add, op1=ALU.add).then_inc(s_residual1, 1)

                def chunk_stats(g):
                    n[0] += 1
                    nc.vector.bn_stats(stats[:, g, :], tok_h[0:CH, g * GTOK:(g + 1) * GTOK]).then_inc(s_dve_chain, 1)

                for g in range(2, GROUPS + 2):
                    if g <= GROUPS:
                        normalise(b, g - 1, link)
                    if g < GROUPS:
                        shift(b, g, link)
                    residual(g - 2)
                    if g < GROUPS:
                        v_blocks(b, g)
                    dve.wait_ge(s_residual1, b * 8 + g - 1)
                    chunk_stats(g - 2)

                def group_norm(i):
                    wait_apart(dve, s_dve_chain, b * CHAIN + n[0])
                    nc.vector.bn_aggr(mv, stats.rearrange("p c s -> p (c s)")).then_inc(s_gn_request, 1)
                    dve.wait_ge(s_gn_request, b * 6 + 2 * i + 1)
                    dve.wait_ge(s_gn_mean, b * 6 + 2 * i + 1)
                    link(nc.vector.tensor_copy(gd[:, 1:2], PS[0:CH, 6, 0:1]))
                    link(nc.vector.tensor_tensor(gd[:, 0:1], mv[:, 0:1], gd[:, 1:2], ALU.subtract))
                    nc.vector.scalar_tensor_tensor(out=ge[:, 0:1], in0=gd[:, 0:1], scalar=gd[:, 0:1],
                                                   in1=mv[:, 1:2], op0=ALU.mult, op1=ALU.add).then_inc(s_gn_request, 1)
                    dve.wait_ge(s_gn_mean, b * 6 + 2 * i + 2)
                    nc.vector.tensor_scalar(gt[:, 0:1], PS[0:CH, 6, 0:1], 1e-5, None, ALU.add)\
                      .then_inc(s_pow_request, 1)
                    dve.wait_ge(s_pow_done, b * 3 + i + 1)
                    link(nc.vector.tensor_tensor(gA[:, 0:1], gp[:, 0:1], gn_w[i], ALU.mult))
                    link(nc.vector.tensor_tensor(ge[:, 1:2], gd[:, 1:2], gA[:, 0:1], ALU.mult))
                    nc.vector.tensor_tensor(gB[:, 0:1], gn_b[i], ge[:, 1:2], ALU.subtract).then_inc(s_gn_affine, 1)

                group_norm(0)
                for g in range(GROUPS):
                    if g % 4 == 0:
                        dve.wait_ge(s_h_ready, b * 2 + g // 4 + 1)
                    chunk_stats(g)
                group_norm(1)
                for c in range(8):
                    sl = slice(c * GTOK, (c + 1) * GTOK)
                    dve.wait_ge(s_mlp2, b * 8 + c + 1)
                    nc.vector.scalar_tensor_tensor(out=tok_h[0:CH, sl], in0=PS[0:CH, 4 + c % 2, 0:GTOK], scalar=b2c,
                                                   in1=tok_h[0:CH, sl], op0=ALU.add, op1=ALU.add)\
                                                     .then_inc(s_residual2, 1)
                    dve.wait_ge(s_residual2, b * 8 + c + 1)
                    chunk_stats(c)
                group_norm(2)

                dve.wait_ge(s_out_written[0], b * 16 + 16)
                for c in range(5):
                    if c < 4:
                        dve.wait_ge(s_piece_h, b * 4 + c + 1)
                        nc.vector.tensor_tensor(pair(tok_h, c), PS[:, 2 * c:2 * c + 2, 0:GTOK], pair(pieces[0], c),
                                                ALU.subtract).then_inc(s_rest, 1)
                    if c >= 1:
                        sl = slice((c - 1) * PAIR, c * PAIR)
                        dve.wait_ge(s_piece_m, b * 4 + c)
                        nc.vector.tensor_tensor(pieces[2][:, sl], tok_h[:, sl], pieces[1][:, sl], ALU.subtract)\
                          .then_inc(s_piece_l, 1)
                for k, (t0, t1) in enumerate(((0, 16), (16, TILES))):
                    dve.wait_ge(s_gv, b * 2 + k + 1)
                    nc.vector.tensor_copy(
                        v_all[:, :, t0:t1, 0:D1].rearrange("p h t c -> p t h c"),
                        PS[:, 2 * k:2 * k + 2, :].rearrange("p a n -> p (a n)")[:, 0:(t1 - t0) * CH]
                        .rearrange("p (t h c) -> p t h c", h=H1, c=D1)).then_inc(s_v_all_ready, 1)

                def take_maxima(r0, r1):
                    for r in range(r0, r1):
                        stage, tile, chunk = MAXIMA[r]
                        t0, t1 = STAGE_TILES[stage % 2]
                        dve.wait_ge(s_slot_filled, b * RING + r + 1)
                        if tile is None:
                            if stage > 0:
                                dve.wait_ge(s_shift_loaded, (b * STAGES + stage) * 48)
                            nc.vector.tensor_copy(neg_rows[0:3 * (t1 - t0), :],
                                                  PS[0:3 * (t1 - t0), 5 + r % 3, 0:64].bitcast(bf16))\
                                                    .then_inc(s_slot_emptied, 1)
                            continue
                        n_ = tile * GROUPS + chunk
                        nc.vector.reduce_max(max_parts[:, n_:n_ + 1], PS[:, 5 + r % 3, 0:GTOK], axis=AX.X)\
                          .then_inc(s_slot_emptied, 1)
                        if (tile, chunk) == (t1 - 1, GROUPS - 1):
                            dve.wait_ge(s_slot_emptied, b * RING + r + 1)
                            shift_pieces(stage)

                def shift_pieces(stage):
                    m = [0]
                    t0, t1 = STAGE_TILES[stage % 2]
                    nt = t1 - t0

                    def step(ins):
                        m[0] += 1
                        ins.then_inc(s_shift_chain, 1)
                        dve.wait_ge(s_shift_chain, (b * STAGES + stage) * 5 + m[0])

                    parts = 2 if stage == 0 else GROUPS
                    step(nc.vector.tensor_reduce(neg_max[:, t0:t1], max_parts[:, t0 * GROUPS:t1 * GROUPS]
                                                 .rearrange("p (t q) -> p t q", q=GROUPS)[:, :, 0:parts], op=ALU.max,
                                                 axis=AX.X, negate=True))
                    step(nc.vector.tensor_copy(neg_pieces[:, 0:nt], neg_max[:, t0:t1]))
                    step(nc.vector.tensor_tensor(neg_rest[:, t0:t1], neg_max[:, t0:t1], neg_pieces[:, 0:nt],
                                ALU.subtract))
                    step(nc.vector.tensor_copy(neg_pieces[:, nt:2 * nt], neg_rest[:, t0:t1]))
                    step(nc.vector.tensor_tensor(neg_rest[:, t0:t1], neg_rest[:, t0:t1], neg_pieces[:, nt:2 * nt],
                                ALU.subtract))
                    nc.vector.tensor_copy(neg_pieces[:, 2 * nt:3 * nt], neg_rest[:, t0:t1]).then_inc(s_max_pieces, 1)

                def copy_half(stage):
                    dve.wait_ge(s_pv_done, (b * STAGES + stage + 1) * EXP_UNITS)
                    if stage == 0:
                        for k in range(H1):
                            dve.wait_ge(s_stacks[k], b * 192 + 192)
                    if stage >= 2:
                        dve.wait_ge(s_out_stored, (b * STAGES + stage - 1) * 64)
                    nc.vector.tensor_copy(o_st[:, stage % 2, :], PS[:, 4, 0:GTOK]).then_inc(s_out_copied, 1)

                def invert_sums(half):
                    dve.wait_ge(s_den_loaded, b * 32 + half * 16 + 16)
                    nc.vector.reciprocal(inv_compact, sums_compact).then_inc(s_den_inverted, 1)

                def scale_att(half):
                    dve.wait_ge(s_att_loaded, b * 32 + half * 16 + 16)
                    dve.wait_ge(s_rden_loaded, b * 128 + half * 64 + 64)
                    for c in range(2):
                        sl = slice(c * PAIR, (c + 1) * PAIR)
                        nc.vector.tensor_tensor(att[half][:, sl], att[half][:, sl], inv_sums[half][:, sl], ALU.mult)\
                          .then_inc(s_att_scaled, 1)

                def add_residual(half):
                    for j in range(4):
                        g = 4 * half + j
                        dve.wait_ge(s_final_proj, b * 8 + g + 1)
                        nc.vector.tensor_tensor(
                            result[half][:, j * GTOK:(j + 1) * GTOK].rearrange("c (i w j) -> c w i j", i=WIN, j=WIN),
                            PS[0:CH, att_bank(g), 0:GTOK].rearrange("c (w i j) -> c w i j", i=WIN, j=WIN),
                            z_w[:, g * GTOK:(g + 1) * GTOK].rearrange("c (w i j) -> c w i j", i=WIN, j=WIN),
                            ALU.add).then_inc(s_final, 1)

                for i in range(FIRST_QUADS):
                    dve.wait_ge(s_quad_filled, b * FIRST_QUADS + i + 1)
                    n_, bank = i // 2 * GROUPS + i % 2, (4, 0)[i % 2]
                    nc.vector.tensor_reduce(max_parts[:, n_:n_ + 1], PS[:, bank:bank + 4, 0:GTOK],
                                            op=ALU.max, axis=AX.XY)\
                      .then_inc(s_quad_emptied, 1)
                dve.wait_ge(s_quad_emptied, (b + 1) * FIRST_QUADS)
                shift_pieces(0)
                taken = 0
                for stage in range(STAGES):
                    until = maxima_before((stage + 1) * EXP_UNITS + PV_LAG) - EARLY * (stage < STAGES - 2)
                    take_maxima(taken, until)
                    taken = until
                    if stage < STAGES - 1:
                        copy_half(stage)
                for g in range(GROUPS):
                    if g == 6:
                        invert_sums(0)
                    square_qk(b + 1, g)
                bound_sums(b + 1)
                scale_att(0)
                invert_norms(b + 1)
                add_residual(0)
                normalise_qk(b + 1)
                copy_half(STAGES - 1)
                shift(b + 1, 0, link)
                v_blocks(b + 1, 0)
                invert_sums(1)
                normalise(b + 1, 0, link)
                shift(b + 1, 1, link)
                v_blocks(b + 1, 1)
                assert n[0] == CHAIN + first_n[0], n[0]
                scale_att(1)
                add_residual(1)

        @block.tensor
        def _(pe):
            mm = nc.tensor.matmul
            pe.wait_ge(s_weights, 16 * NLOAD)
            pe.wait_ge(s_onehot, 2)
            hot = [tok_qk[:, 0:WTOK * WTOK], scores_buf[:, :, :].rearrange("p a n -> p (a n)")[:, 0:WTOK * WTOK]]
            NB = WTOK * WTOK // 7
            for c in range(7):
                sl = slice(c * NB, (c + 1) * NB)
                mm(PS[0:H0, c, 0:NB], bias_table[:, 0, :], hot[0][:, sl], start=True, stop=False)
                mm(PS[0:H0, c, 0:NB], bias_table[0:TABLE - 128, 1, :], hot[1][0:TABLE - 128, sl], start=False,
                            stop=True)\
                    .then_inc(s_bias_product, 1)
            mm(PS[0:CH, 7, 0:1], w_p0c[:], bv0, start=True, stop=True).then_inc(s_bias_product, 1)
            pe.wait_ge(s_setup, 2)
            pe.wait_ge(s_bias_copied, 7)
            pe.wait_ge(s_zeroed, 9)

            def product_qk(t, g):
                pe.wait_ge(s_x_by_windows, t * 8 + g + 1)
                if g >= 3:
                    pe.wait_ge(s_qk_biased, t * 8 + g - 2)
                mm(PS[:, SIDE_BANKS[g], 0:GTOK], w_qk0[:], x_w[:, g * GTOK:(g + 1) * GTOK], start=True, stop=True)\
                    .then_inc(s_qk_product, 1)

            def sum_heads(t, r):
                pe.wait_ge(s_qk_biased, t * 8 + 6 + r)
                pe.wait_ge(s_qk_squares, t * 8 + 4 * r + 4)
                for j in range(4):
                    g = 4 * r + j
                    last = mm(PS[32 * j:32 * j + 32, SIDE_BANKS[8 + r], 0:GTOK], w_head_sum[:],
                              tok_h[:, g * GTOK:(g + 1) * GTOK], start=True, stop=True)
                last.then_inc(s_head_sums, 1)

            def spread_norms(t, g):
                pe.wait_ge(s_norms_inverted, t * 2 + g // 4 + 1)
                if g >= 3:
                    pe.wait_ge(s_qk_normalised, t * 8 + g - 2)
                mm(PS[:, SIDE_BANKS[14 + g], 0:GTOK], w_spread[:, g % 4, :],
                   tok_h[:, (g // 4) * GTOK:(g // 4 + 1) * GTOK], start=True, stop=True).then_inc(s_norms_spread, 1)

            def scores(t, g):
                pe.wait_ge(s_queries[g % 2], t * 64 + (g // 2 + 1) * 16)
                if g == 0:
                    wait_apart(pe, s_qk_normalised, t * 8 + 8)
                else:
                    wait_apart(pe, s_win_shifted, t * 8 + g)
                for w in range(8):
                    q0, m = g * GTOK + w * WTOK, (64, WTOK)[w == 7]
                    last = mm(PS[64 * (w % 2):64 * (w % 2) + m, w // 2, 0:GTOK], tok_unit[0:CH + WTOK, q0:q0 + m],
                              kmask[0:CH + WTOK, g % 2, :, w * WTOK:(w + 1) * WTOK], start=True, stop=True)
                last.then_inc(s_win_scores, 1)

            def values(t, g):
                if g >= 1:
                    pe.wait_ge(s_win_v_blocks, t * 8 + g)
                pe.wait_ge(s_x_twice, t * 8 + g + 1)
                for w in range(8):
                    last = mm(PS[0:2 * WTOK, 6, w * CH:(w + 1) * CH],
                              x_tw[:, g % 2, w, :, :].rearrange("c a m -> c (a m)"), w_v0[:],
                              start=True, stop=True)
                last.then_inc(s_win_v, 1)

            def transpose(t, g, half):
                pe.wait_ge(s_win_probs, t * 8 + g + 1)
                if 2 * g + half >= 1:
                    pe.wait_ge(s_win_transposed_copied, t * 16 + 2 * g + half)
                for p in range(2):
                    for q in range(4):
                        c0 = (2 * half + p) * GTOK + q * 2 * WTOK
                        last = nc.tensor.transpose(PS[0:2 * WTOK, 4 + p, q * 128:(q + 1) * 128],
                                                   win_scores[:, g % 2, c0:c0 + 2 * WTOK], ident_f32[:])
                last.then_inc(s_win_transposed, 1)

            def attend(t, g):
                pe.wait_ge(s_win_v_blocks, t * 8 + g + 1)
                if g >= 1:
                    pe.wait_ge(s_residual1, t * 8 + g)
                for w in range(8):
                    if w % 4 == 0:
                        pe.wait_ge(s_win_transposed_copied, t * 16 + 2 * g + w // 4 + 1)
                    for q in range(4):
                        c0 = q * 128 + 64 * (w % 2)
                        last = mm(PS[32 * q:32 * q + 32, 7, w * WTOK:(w + 1) * WTOK], win_v[:, g % 2, w, q, :],
                                  win_probs_t[0:2 * WTOK, g % 2, w // 2, c0:c0 + WTOK], start=True, stop=True)
                last.then_inc(s_win_pv, 1)

            def first_groups(t):
                scores(t, 0)
                values(t, 0)
                scores(t, 1)
                if not isinstance(t, int):
                    wait_apart(pe, s_out_copied, t * STAGES)
                transpose(t, 0, 0)
                values(t, 1)
                transpose(t, 0, 1)
                attend(t, 0)

            pe.wait_ge(s_final, 1)
            pe.wait_ge(s_bias_loaded, 14 * 16)
            for half in range(2):
                pe.wait_ge(s_out_written[half], 16)
            pe.wait_ge(s_setup, 3)
            for g in range(GROUPS):
                product_qk(0, g)
            for r in range(2):
                sum_heads(0, r)
            for g in range(GROUPS):
                spread_norms(0, g)
            first_groups(0)
            with pe.Fori(0, IMAGES) as b:
                pe.wait_ge(s_final, b * 8 + 1)

                def project(g):
                    pe.wait_ge(s_win_att, b * 8 + g + 1)
                    mm(PS[0:CH, 7, 0:GTOK], w_p0[:], tok_qk[:, g * GTOK:(g + 1) * GTOK], start=True, stop=True)\
                        .then_inc(s_win_proj, 1)

                for g in range(2, GROUPS + 2):
                    if g < GROUPS:
                        scores(b, g)
                    project(g - 2)
                    if g <= GROUPS:
                        transpose(b, g - 1, 0)
                    if g < GROUPS:
                        values(b, g)
                    if g <= GROUPS:
                        transpose(b, g - 1, 1)
                        attend(b, g - 1)

                def group_mean_of(i):
                    wait_apart(pe, s_gn_request, b * 6 + 2 * i + 1)
                    mm(PS[0:CH, 6, 0:1], w_group_mean[:], mv[:, 0:1], start=True, stop=True).then_inc(s_gn_mean, 1)
                    wait_apart(pe, s_gn_request, b * 6 + 2 * i + 2)
                    mm(PS[0:CH, 6, 0:1], w_group_mean[:], ge[:, 0:1], start=True, stop=True).then_inc(s_gn_mean, 1)

                group_mean_of(0)
                group_mean_of(1)
                for c in range(9):
                    if c < 8:
                        pe.wait_ge(s_mlp_in, b * 2 + c // 4 + 1)
                        if c >= 2:
                            pe.wait_ge(s_hidden, b * 16 + 2 * c - 2)
                        for e in range(2):
                            last = mm(PS[:, 2 * (c % 2) + e, 0:GTOK], w_1[:, 128 * e:128 * e + 128],
                                      tok_qk[0:CH, c * GTOK:(c + 1) * GTOK], start=True, stop=True)
                        last.then_inc(s_mlp1, 1)
                    if c >= 1:
                        k = c - 1
                        pe.wait_ge(s_hidden, b * 16 + 2 * c)
                        if k >= 2:
                            pe.wait_ge(s_residual2, b * 8 + k - 1)
                        for e in range(2):
                            last = mm(PS[0:CH, 4 + k % 2, 0:GTOK], w_2[:, e, :], hidden[:, 2 * (k % 2) + e, 0:GTOK],
                                      start=(e == 0), stop=(e == 1))
                        last.then_inc(s_mlp2, 1)
                group_mean_of(2)

                for c in range(4):
                    if c % 2 == 0:
                        pe.wait_ge(s_z_ready, b * 2 + c // 2 + 1)
                    for i in range(2):
                        g = 2 * c + i
                        last = mm(PS[:, g, 0:GTOK], w_qk1[:], z_w[:, g * GTOK:(g + 1) * GTOK], start=True, stop=True)
                    last.then_inc(s_gqk, 1)
                for t in range(TILES):
                    if t % 16 == 0:
                        pe.wait_ge(s_rest, b * 4 + t // 16 + 1)
                    last = mm(PS[:, t // 8, (t % 8) * CH:(t % 8 + 1) * CH], z_w[:, t * 128:(t + 1) * 128], w_v1[:],
                              start=True, stop=True)
                    if t in (15, TILES - 1):
                        last.then_inc(s_gv, 1)

                def maxima(r0, r1):
                    for r in range(r0, r1):
                        stage, tile, chunk = MAXIMA[r]
                        h, (t0, t1) = stage // 2, STAGE_TILES[stage % 2]
                        if tile == 0 and chunk == 0:
                            pe.wait_ge(s_stacks[h], b * 192 + 192)
                        if r >= 3:
                            pe.wait_ge(s_slot_emptied, b * RING + r - 2)
                        if tile is None:
                            wait_apart(pe, s_max_pieces, b * STAGES + stage + 1)
                            nc.tensor.transpose(PS[0:3 * (t1 - t0), 5 + r % 3, 0:64].bitcast(bf16),
                                                neg_pieces[:, 0:3 * (t1 - t0)], ident_bf16[:])\
                                                  .then_inc(s_slot_filled, 1)
                        else:
                            mm(PS[:, 5 + r % 3, 0:GTOK], q_stack[0:STACK, h, tile * 128:(tile + 1) * 128],
                               k_stack[0:STACK, h, chunk * GTOK:(chunk + 1) * GTOK], start=True, stop=True)\
                                 .then_inc(s_slot_filled, 1)

                def project_att(g):
                    if g == 0:
                        pe.wait_ge(s_qk_biased, (b + 1) * 8 + 8)
                    elif g <= 2:
                        pe.wait_ge(s_sums_bounded, (b + 1) * 2 + g)
                    elif g == 3:
                        pe.wait_ge(s_final, b * 8 + 2)
                    elif g == 4:
                        pe.wait_ge(s_win_transposed_copied, (b + 1) * 16 + 2)
                    elif g >= 6:
                        pe.wait_ge(s_final, b * 8 + g)
                    wait_apart(pe, s_att_scaled, b * 4 + g // 2 + 1)
                    mm(PS[0:CH, att_bank(g), 0:GTOK], w_p1[:], att[g // 4][:, (g % 4) * GTOK:(g % 4 + 1) * GTOK],
                       start=True, stop=True).then_inc(s_final_proj, 1)

                def side_product(v):
                    if v == 2:
                        pe.wait_ge(s_slot_emptied, (b + 1) * RING)
                    if v < 18 and v % 2 == 0:
                        product_qk(b + 1, v // 2 - 1)
                    elif v in (19, 20):
                        sum_heads(b + 1, v - 19)
                    elif 26 <= v < 34 and v % 2 == 0:
                        project_att((v - 26) // 2)
                    elif 34 <= v < 50 and v % 2 == 0:
                        if v == 34:
                            pe.wait_ge(s_final, b * 8 + 5)
                        spread_norms(b + 1, (v - 34) // 2)

                pe.wait_ge(s_rest, b * 4 + 4)
                pe.wait_ge(s_v_all_ready, b * 2 + 2)
                pe.wait_ge(s_stacks[0], b * 192 + 192)
                for i in range(FIRST_QUADS):
                    tile, bank = i // 2, (4, 0)[i % 2]
                    if i >= 2:
                        pe.wait_ge(s_quad_emptied, b * FIRST_QUADS + i - 1)
                    for j in range(4):
                        chunk = 4 * (i % 2) + j
                        last = mm(PS[:, bank + j, 0:GTOK], q_stack[0:STACK, 0, tile * 128:(tile + 1) * 128],
                                  k_stack[0:STACK, 0, chunk * GTOK:(chunk + 1) * GTOK], start=True, stop=True)
                    last.then_inc(s_quad_filled, 1)
                pe.wait_ge(s_quad_emptied, (b + 1) * FIRST_QUADS - 1)
                maxima(0, MAX_LEAD)
                pe.wait_ge(s_ones_set, b * 2 + 2)
                done = MAX_LEAD
                for u in range(STAGES * EXP_UNITS + PV_LAG):
                    until = maxima_before(u + 1)
                    if u < STAGES * EXP_UNITS:
                        stage, kt, i = u // EXP_UNITS, (u % EXP_UNITS) // 2, u % 2
                        h, half = stage // 2, stage % 2
                        if kt == 0 and i == 0:
                            pe.wait_ge(s_shift_loaded, (b * STAGES + stage) * 48 + 48)
                        if u >= 2:
                            pe.wait_ge(s_exps, b * STAGES * EXP_UNITS + u - 1)
                        for j in range(2):
                            c = 4 * half + 2 * i + j
                            last = mm(PS[:, 2 * (u % 2) + j, 0:GTOK],
                                      k_stack[0:STACK + SHIFT, h, kt * 128:(kt + 1) * 128],
                                      q_stack[0:STACK + SHIFT, h, c * GTOK:(c + 1) * GTOK], start=True, stop=True)
                        last.then_inc(s_scores, 1)
                    maxima(done, max(done, until - 1))
                    if u >= PV_LAG:
                        k = u - PV_LAG
                        stage, kt, i = k // EXP_UNITS, (k % EXP_UNITS) // 2, k % 2
                        pe.wait_ge(s_exps, b * STAGES * EXP_UNITS + k + 1)
                        if k % EXP_UNITS == 0 and stage > 0:
                            pe.wait_ge(s_out_copied, b * STAGES + stage)
                        for j in range(2):
                            q0 = 32 * (2 * i + j)
                            last = mm(PS[q0:q0 + 32, 4, 0:GTOK], v_all[:, stage // 2, kt, :],
                                      exps[:, k % 4, j * GTOK:(j + 1) * GTOK], start=(kt == 0), stop=(kt == TILES - 1))
                        last.then_inc(s_pv_done, 1)
                    maxima(max(done, until - 1), until)
                    done = until
                    v = u - (STAGES - 1) * EXP_UNITS
                    if v >= 2:
                        side_product(v)
                first_groups(b + 1)
                for g in range(4, GROUPS):
                    project_att(g)


def constants():
    import numpy as np

    head = np.arange(128) // D0
    group = np.arange(CH) // 4
    mask = np.repeat(np.arange(2), WTOK)[:, None] == np.repeat(np.arange(2), D0)[None, :]
    return {
        "ident": np.eye(128, dtype=np.float32),
        "head_sum": (head[:, None] == np.arange(32)[None, :]).astype(np.float32),
        "head_spread": (np.arange(128)[:, None, None] == 32 * np.arange(4)[None, :, None]
                        + head[None, None, :]).astype(np.float32),
        "group_mean": (group[:, None] == group[None, :]).astype(np.float32) / 4,
        "head_mask": mask.astype(np.float32),
        "query_ident": np.tile(np.eye(WTOK, dtype=np.float32), (1, RES // WIN)),
        "rows": np.stack([np.arange(128), np.arange(128) + 128], 1).astype(np.float32),
    }


_ORDER = ["x", "qkv_w", "qkv_b", "logit_scale", "bias_table", "rel_index", "proj_w", "proj_b", "gn1_w", "gn1_b",
          "gn2_w", "gn2_b", "mlp_gn_w", "mlp_gn_b", "mlp_w1", "mlp_b1", "mlp_w2", "mlp_b2"]
_TRANSPOSED = {"qkv_w", "proj_w", "mlp_w1", "mlp_w2"}


def kernel(**inputs):
    import numpy as np
    import concourse.bacc as bacc
    from concourse.bass_utils import run_bass_kernel_spmd as run

    given = {"x": np.asarray(inputs["x"]).reshape(IMAGES, CH, TOKENS)}
    for name in _ORDER[1:]:
        a = np.asarray(inputs["L0_conv_" + name])
        given[name] = a.T if name in _TRANSPOSED else a
    for name in ("w_qkv", "w_proj"):
        given[name] = np.asarray(inputs["L1_conv_" + name]).T
    given.update(constants())

    nc = bacc.Bacc("TRN2", target_bir_lowering=False, num_devices=1)
    arrays, args = {}, []
    for name, a in given.items():
        a = np.ascontiguousarray(a)
        arrays["in_" + name] = a
        args.append(nc.dram_tensor("in_" + name, a.shape, mybir.dt.from_np(a.dtype), kind="ExternalInput").ap())
    f32 = mybir.dt.float32
    args.append(nc.dram_tensor("out_0", [IMAGES, CH, TOKENS], f32, kind="ExternalOutput").ap())
    for name, shape in (("scratch_bias", [H0, WTOK * WTOK]), ("scratch_att", [2, H1, D1 + 1, HALF]),
                        ("scratch_rden", [2, H1, HALF])):
        args.append(nc.dram_tensor(name, shape, f32, kind="Internal").ap())
    nc.disable_value_cache = True
    attention_mlp_kernel(nc, *args)
    r = run(nc, [arrays], core_ids=[0])
    return r.results[0]["out_0"].reshape(IMAGES, CH, RES, RES)
```
